# Optimizing a Trainium2 kernel written in Bass

```python
import numpy as np
import jax
import jax.numpy as jnp

def _softmax(x, axis=-1):
    return jax.nn.softmax(x, axis=axis)

def _gelu(x):
    return jax.nn.gelu(x, approximate=True)

def _silu(x):
    return jax.nn.silu(x)

def _sigmoid(x):
    return jax.nn.sigmoid(x)

def _layernorm(x, axis=-1, eps=1e-05):
    m = jnp.mean(x, axis=axis, keepdims=True)
    v = jnp.var(x, axis=axis, keepdims=True)
    return (x - m) / jnp.sqrt(v + eps)

def _scatter_add(tgt, idx, src, axis=0):
    return tgt.at[idx].add(src)

def _segment_sum(src, seg, n):
    return jax.ops.segment_sum(src, seg, n)
kernel_name = 'mk_flamingo_gated_d1_seqx_r4_4faa87'

def setup_inputs(seed: int=0):
    np.random.seed(seed)
    _w = jnp.asarray

    def _rec_inputs():
        import jax
        import jax.numpy as jnp
        _rk = jax.random.key(seed)
        x = 7.22e-05 + 1 * jax.random.normal(jax.random.fold_in(_rk, 1), (8, 512, 256), jnp.float32)
        _lenS = 512 - jax.random.randint(jax.random.fold_in(_rk, 7), (8,), 0, max(1, 512 // 4) + 1, jnp.int32)
        _lenS2 = 512 - jax.random.randint(jax.random.fold_in(_rk, 8), (8,), 0, max(1, 512 // 4) + 1, jnp.int32)
        _ctx_1024P = jax.random.normal(jax.random.fold_in(_rk, 11), (8, 16, 256), jnp.float32)
        _ctx_1024c = jax.random.dirichlet(jax.random.fold_in(_rk, 511), 0.3 * jnp.ones((16,), jnp.float32), (8, 512))
        _ctx_1024t = jnp.einsum('bsk,bkd->bsd', _ctx_1024c, _ctx_1024P)
        _ctx_1024t = _ctx_1024t * jax.lax.rsqrt(jnp.mean(jnp.square(_ctx_1024t)) + 1e-12) * 0.953939
        ctx_1024 = 4.13588e-05 + 0.999923 * (_ctx_1024t + 0.3 * jax.random.normal(jax.random.fold_in(_rk, 611), (8, 512, 256), jnp.float32))
        _g = jax.random.normal(jax.random.fold_in(_rk, 9001), (2, 1), jnp.float32)
        _g = jnp.sign(_g) * jnp.maximum(jnp.abs(_g), 1.0) + (_g == 0) * 1.0
        g_xattn = _g[0]
        g_ffn = _g[1]
        return (x, ctx_1024, g_xattn, g_ffn)
    x, ctx_1024, g_xattn, g_ffn = _rec_inputs()

    def _L0_xattn_setup():
        import jax, jax.numpy as jnp
        import numpy as np
        B, T, D, H = (4, 512, 256, 1024)
        S = 64
        EPS = 1e-05

        def _layer_norm(x, gamma, beta):
            mu = jnp.mean(x, axis=-1, keepdims=True)
            var = jnp.mean(jnp.square(x - mu), axis=-1, keepdims=True)
            return (x - mu) * jax.lax.rsqrt(var + EPS) * gamma + beta

        def _aft_local(emb, wq, bq, wk, bk, wv, bv, wo, bo, pos_bias):
            q = emb @ wq + bq
            k = emb @ wk + bk
            v = emb @ wv + bv
            idx = jnp.arange(T)
            mask = (jnp.abs(idx[:, None] - idx[None, :]) < S).astype(pos_bias.dtype)
            w = pos_bias * mask
            max_k = jnp.max(k, axis=1, keepdims=True)
            max_w = jnp.max(w, axis=1, keepdims=True)
            ek = jnp.exp(k - max_k)
            ew = jnp.exp(w - max_w)
            num = jnp.einsum('tj,bjd->btd', ew, ek * v)
            den = jnp.einsum('tj,bjd->btd', ew, ek)
            y = jax.nn.sigmoid(q) * num / den
            return y @ wo + bo
        key = jax.random.key(seed)
        ks = jax.random.split(key, 16)
        sd = 0.02
        return {'x': jax.random.normal(ks[0], (B, T, D), jnp.float32), 'pos_encod': jax.random.normal(ks[1], (B, T, D), jnp.float32), 'wq': jax.random.normal(ks[2], (D, D), jnp.float32) * sd, 'bq': jnp.zeros((D,), jnp.float32), 'wk': jax.random.normal(ks[3], (D, D), jnp.float32) * sd, 'bk': jnp.zeros((D,), jnp.float32), 'wv': jax.random.normal(ks[4], (D, D), jnp.float32) * sd, 'bv': jnp.zeros((D,), jnp.float32), 'wo': jax.random.normal(ks[5], (D, D), jnp.float32) * sd, 'bo': jnp.zeros((D,), jnp.float32), 'pos_bias': jax.random.normal(ks[6], (T, T), jnp.float32) * sd, 'gamma': jnp.ones((D,), jnp.float32), 'beta': jnp.zeros((D,), jnp.float32), 'w1': jax.random.normal(ks[7], (D, H), jnp.float32) * sd, 'b1': jnp.zeros((H,), jnp.float32), 'w2': jax.random.normal(ks[8], (H, D), jnp.float32) * sd, 'b2': jnp.zeros((D,), jnp.float32)}
    _L0_xattn_all = _L0_xattn_setup()
    _L0_xattn_in = {k: v for k, v in _L0_xattn_all.items() if k in ('wq', 'bq', 'wk', 'bk', 'wv', 'bv', 'wo', 'bo', 'pos_bias', 'gamma', 'beta', 'w1', 'b1', 'w2', 'b2')}
    del _L0_xattn_all

    def _L0_ffn_setup():
        import jax, jax.numpy as jnp
        import numpy as np
        DIM = 256

        def _reference_tuple_inner(x, W_r, W_k, W_v, mu_r, mu_k):
            B, T, C = x.shape
            x_prev = jnp.concatenate([jnp.zeros((B, 1, C), x.dtype), x[:, :-1, :]], axis=1)
            xr = mu_r * x + (1.0 - mu_r) * x_prev
            xk = mu_k * x + (1.0 - mu_k) * x_prev
            r = jax.nn.sigmoid(jnp.einsum('btc,dc->btd', xr, W_r))
            k = jnp.einsum('btc,dc->btd', xk, W_k)
            k_act = jnp.square(jax.nn.relu(k))
            out = r * jnp.einsum('btc,dc->btd', k_act, W_v)
            new_state = x[:, -1, :]
            return (out, new_state)
        key = jax.random.key(seed)
        ks = jax.random.split(key, 6)
        B, T, C = (8, 512, DIM)
        x = jax.random.normal(ks[0], (B, T, C), dtype=jnp.float32)
        s = 1.0 / np.sqrt(C)
        W_r = jax.random.uniform(ks[1], (C, C), jnp.float32, -s, s)
        W_k = jax.random.uniform(ks[2], (C, C), jnp.float32, -s, s)
        W_v = jax.random.uniform(ks[3], (C, C), jnp.float32, -s, s)
        mu_r = jax.random.uniform(ks[4], (C,), jnp.float32)
        mu_k = jax.random.uniform(ks[5], (C,), jnp.float32)
        return {'x': x, 'W_r': W_r, 'W_k': W_k, 'W_v': W_v, 'mu_r': mu_r, 'mu_k': mu_k}
    _L0_ffn_all = _L0_ffn_setup()
    _L0_ffn_in = {k: v for k, v in _L0_ffn_all.items() if k in ('W_r', 'W_k', 'W_v', 'mu_r', 'mu_k')}
    del _L0_ffn_all
    return {'x': x, 'ctx_1024': ctx_1024, 'g_xattn': g_xattn, 'g_ffn': g_ffn, 'L0_xattn_wq': _L0_xattn_in['wq'], 'L0_xattn_bq': _L0_xattn_in['bq'], 'L0_xattn_wk': _L0_xattn_in['wk'], 'L0_xattn_bk': _L0_xattn_in['bk'], 'L0_xattn_wv': _L0_xattn_in['wv'], 'L0_xattn_bv': _L0_xattn_in['bv'], 'L0_xattn_wo': _L0_xattn_in['wo'], 'L0_xattn_bo': _L0_xattn_in['bo'], 'L0_xattn_pos_bias': _L0_xattn_in['pos_bias'], 'L0_xattn_gamma': _L0_xattn_in['gamma'], 'L0_xattn_beta': _L0_xattn_in['beta'], 'L0_xattn_w1': _L0_xattn_in['w1'], 'L0_xattn_b1': _L0_xattn_in['b1'], 'L0_xattn_w2': _L0_xattn_in['w2'], 'L0_xattn_b2': _L0_xattn_in['b2'], 'L0_ffn_W_r': _L0_ffn_in['W_r'], 'L0_ffn_W_k': _L0_ffn_in['W_k'], 'L0_ffn_W_v': _L0_ffn_in['W_v'], 'L0_ffn_mu_r': _L0_ffn_in['mu_r'], 'L0_ffn_mu_k': _L0_ffn_in['mu_k']}

def reference(x, ctx_1024, g_xattn, g_ffn, L0_xattn_wq, L0_xattn_bq, L0_xattn_wk, L0_xattn_bk, L0_xattn_wv, L0_xattn_bv, L0_xattn_wo, L0_xattn_bo, L0_xattn_pos_bias, L0_xattn_gamma, L0_xattn_beta, L0_xattn_w1, L0_xattn_b1, L0_xattn_w2, L0_xattn_b2, L0_ffn_W_r, L0_ffn_W_k, L0_ffn_W_v, L0_ffn_mu_r, L0_ffn_mu_k):
    import jax
    import jax.numpy as jnp

    def _L0_xattn_ref(x, pos_encod, wq, bq, wk, bk, wv, bv, wo, bo, pos_bias, gamma, beta, w1, b1, w2, b2):
        import jax, jax.numpy as jnp
        import numpy as np
        B, T, D, H = (4, 512, 256, 1024)
        S = 64
        EPS = 1e-05

        def _layer_norm(x, gamma, beta):
            mu = jnp.mean(x, axis=-1, keepdims=True)
            var = jnp.mean(jnp.square(x - mu), axis=-1, keepdims=True)
            return (x - mu) * jax.lax.rsqrt(var + EPS) * gamma + beta

        def _aft_local(emb, wq, bq, wk, bk, wv, bv, wo, bo, pos_bias):
            q = emb @ wq + bq
            k = emb @ wk + bk
            v = emb @ wv + bv
            idx = jnp.arange(T)
            mask = (jnp.abs(idx[:, None] - idx[None, :]) < S).astype(pos_bias.dtype)
            w = pos_bias * mask
            max_k = jnp.max(k, axis=1, keepdims=True)
            max_w = jnp.max(w, axis=1, keepdims=True)
            ek = jnp.exp(k - max_k)
            ew = jnp.exp(w - max_w)
            num = jnp.einsum('tj,bjd->btd', ew, ek * v)
            den = jnp.einsum('tj,bjd->btd', ew, ek)
            y = jax.nn.sigmoid(q) * num / den
            return y @ wo + bo
        emb = x + pos_encod
        attn = _aft_local(emb, wq, bq, wk, bk, wv, bv, wo, bo, pos_bias)
        a = _layer_norm(attn + emb, gamma, beta)
        ff = jax.nn.relu(a @ w1 + b1) @ w2 + b2
        return _layer_norm(ff + a, gamma, beta)

    def _L0_ffn_ref(x, W_r, W_k, W_v, mu_r, mu_k):
        import jax, jax.numpy as jnp
        import numpy as np
        DIM = 256

        def _reference_tuple_inner(x, W_r, W_k, W_v, mu_r, mu_k):
            B, T, C = x.shape
            x_prev = jnp.concatenate([jnp.zeros((B, 1, C), x.dtype), x[:, :-1, :]], axis=1)
            xr = mu_r * x + (1.0 - mu_r) * x_prev
            xk = mu_k * x + (1.0 - mu_k) * x_prev
            r = jax.nn.sigmoid(jnp.einsum('btc,dc->btd', xr, W_r))
            k = jnp.einsum('btc,dc->btd', xk, W_k)
            k_act = jnp.square(jax.nn.relu(k))
            out = r * jnp.einsum('btc,dc->btd', k_act, W_v)
            new_state = x[:, -1, :]
            return (out, new_state)
        return _reference_tuple_inner(x, W_r, W_k, W_v, mu_r, mu_k)[0]
    x = x + jnp.tanh(g_xattn[0]) * _L0_xattn_ref(_layernorm(x, axis=-1), ctx_1024, L0_xattn_wq, L0_xattn_bq, L0_xattn_wk, L0_xattn_bk, L0_xattn_wv, L0_xattn_bv, L0_xattn_wo, L0_xattn_bo, L0_xattn_pos_bias, L0_xattn_gamma, L0_xattn_beta, L0_xattn_w1, L0_xattn_b1, L0_xattn_w2, L0_xattn_b2)
    x = x + jnp.tanh(g_ffn[0]) * _L0_ffn_ref(_layernorm(x, axis=-1), L0_ffn_W_r, L0_ffn_W_k, L0_ffn_W_v, L0_ffn_mu_r, L0_ffn_mu_k)
    return x

_drawn_inputs = setup_inputs


def setup_inputs(seed=0):
    import zlib

    import numpy as np

    out = dict(_drawn_inputs(seed))
    spreads = {'L0_xattn_bq': (0.0, 0.8),
     'L0_xattn_bk': (0.0, 2.0),
     'L0_xattn_bv': (0.0, 0.8),
     'L0_xattn_bo': (0.0, 0.409),
     'L0_xattn_gamma': (1.0, 0.2),
     'L0_xattn_beta': (0.0, 0.1),
     'L0_xattn_b1': (0.0, 0.449),
     'L0_xattn_b2': (0.0, 0.1)}
    factors = {'L0_xattn_wq': 8.0,
     'L0_xattn_wk': 8.0,
     'L0_xattn_wv': 6.059,
     'L0_xattn_wo': 5.14,
     'L0_xattn_pos_bias': 34.888,
     'L0_ffn_W_r': 5.358,
     'L0_ffn_mu_r': 8.0}
    for name, (base, spread) in spreads.items():
        noise = np.random.default_rng([zlib.crc32(name.encode()), seed]).standard_normal(out[name].shape)
        drawn = base * np.exp(spread * noise) if base else spread * noise
        out[name] = jnp.asarray(drawn.astype(out[name].dtype))
    for name, factor in factors.items():
        out[name] = (out[name] * factor).astype(out[name].dtype)
    return out
```

```python
from contextlib import ExitStack

import concourse.bass as bass
from concourse import mybir

F32 = mybir.dt.float32
F32R = mybir.dt.float32r
ALU = mybir.AluOpType
ACT = mybir.ActivationFunctionType
AX_X = mybir.AxisListType.X

P = 128
BATCH = 8
T = 512
D = 256
H = 1024
BAND = 64
EPS = 1e-5
TT = T // P
DC = D // P
HC = H // P
NQ = HC // 2
PAIR = 1024
HD = 6
NU = 8

C_BQ, C_BK, C_BV, C_GAMMA, C_BETA, C_MUR, C_MUK, C_B1 = 0, 2, 4, 6, 8, 10, 12, 14
C_GX = C_B1 + HC
C_GF = C_GX + 1
NVEC = C_GF + 1


def flamingo_gated_block(nc, A_x, A_ctx, A_vec, A_rows, A_bias, A_pos, A_wk, A_wq, A_wv, A_wo,
                         A_w1, A_w2, A_fk, A_fr, A_fv, out):
    ctx = ExitStack()
    with ctx:
        def sb(name, cols, dt=F32):
            return ctx.enter_context(nc.sbuf_tensor(name, [P, cols], dt))[:, :]

        def sem(name):
            return ctx.enter_context(nc.semaphore(name))

        ident = sb("ident", P)
        ident_r = sb("ident_r", P, F32R)
        ones_r = sb("ones_r", P, F32R)
        vec = sb("vec", NVEC)
        half_bq = sb("half_bq", DC)
        gates = sb("gates", 3)
        gamma_t = sb("gamma_t", D)
        beta_t = sb("beta_t", D)
        bias_f = sb("bias_f", 2 * D)
        bias_r = sb("bias_r", 2 * D, F32R)
        minus_half, minus_one, eps_col = sb("minus_half", TT), sb("minus_one", TT), sb("eps_col", TT)
        unit_cols = [PAIR] * (NU - 1) + [DC * D]
        w_hi = [sb(f"w_hi{u}", unit_cols[u], F32R) for u in range(NU)]
        w_lo = [sb(f"w_lo{u}", unit_cols[u], F32R) for u in range(NU)]
        ew_hi = sb("ew_hi", TT * T, F32R)
        ew_lo = sb("ew_lo", TT * T, F32R)
        pos_nmax = sb("pos_nmax", TT)

        x_in = [sb(f"x_in{p}", TT * D) for p in range(2)]
        emb = [sb(f"emb{p}", TT * D) for p in range(2)]
        norm = sb("norm", TT * D)
        emb_hi, emb_lo = sb("emb_hi", DC * T, F32R), sb("emb_lo", DC * T, F32R)
        ek_t = sb("ek_t", DC * T)
        val = sb("val", TT * D)
        gate_q = sb("gate_q", DC * T)
        ek_hi, ek_lo = sb("ek_hi", TT * D, F32R), sb("ek_lo", TT * D, F32R)
        ev_hi, ev_lo = sb("ev_hi", TT * D, F32R), sb("ev_lo", TT * D, F32R)
        y = sb("y", DC * T)
        ya_hi, ya_lo = sb("ya_hi", DC * T, F32R), sb("ya_lo", DC * T, F32R)
        res = sb("res", TT * D)
        hid = [sb(f"hid{r}", PAIR) for r in range(2)]
        hid_hi = [sb(f"hid_hi{r}", PAIR, F32R) for r in range(2)]
        hid_lo = [sb(f"hid_lo{r}", PAIR, F32R) for r in range(2)]
        x_beta = sb("x_beta", TT * D)
        x1 = sb("x1", TT * D)
        xn_t = sb("xn_t", DC * (T + 1))
        delta = sb("delta", DC * T)
        xk = sb("xk", DC * T)
        xr = hid[0]
        out_sb = sb("out_sb", TT * D)
        xk_hi, xk_lo = hid_hi[1], hid_lo[1]
        xr_hi, xr_lo = hid_hi[0], hid_lo[0]
        stage = [hid[0], hid[1], x1, out_sb]
        UNIT_STAGE = [0, 1, 0, 1, 2, 3, 2, 3]

        KINDS = ("head", "mid", "ff", "fin")
        st = {k: sb(f"st_{k}", TT * HD) for k in KINDS}
        mv = {k: sb(f"mv_{k}", TT * 2) for k in KINDS}
        ve = {k: sb(f"ve_{k}", TT) for k in KINDS}
        nm = {k: sb(f"nm_{k}", TT) for k in KINDS}
        rs = {k: sb(f"rs_{k}", TT) for k in KINDS}
        nmr = {k: sb(f"nmr_{k}", TT) for k in KINDS}
        held = sb("held", 1)
        kmax, kshift, kbias = sb("kmax", DC), sb("kshift", DC), sb("kbias", DC)

        ps = ctx.enter_context(nc.psum_tensor("ps", [P, 4 * PAIR], F32))

        def bank(pair, b=0, n=512):
            o = pair * PAIR + 512 * b
            return ps[:, o:o + n]

        def pair(k):
            return ps[:, k * PAIR:(k + 1) * PAIR]

        x_landed, out_stored = sem("x_landed"), sem("out_stored")
        vec_landed, rows_landed = sem("vec_landed"), sem("rows_landed")
        unit_landed = [sem(f"unit_landed{u}") for u in range(NU)]
        pos_landed = [sem(f"pos_landed{u}") for u in range(2)]
        ident_set, const_set, dve_const, act_const = sem("ident_set"), sem("const_set"), sem("dve_const"), sem("act_const")
        w_hi_done, w_lo_done = sem("w_hi_done"), sem("w_lo_done")
        pos_masked, pos_max_done, pos_exp_done = sem("pos_masked"), sem("pos_max_done"), sem("pos_exp_done")
        pos_turned, ew_hi_done, ew_lo_done = sem("pos_turned"), sem("ew_hi_done"), sem("ew_lo_done")
        st_done = {k: sem(f"st_{k}_done") for k in KINDS}
        mv_done = {k: sem(f"mv_{k}_done") for k in KINDS}
        ve_done = {k: sem(f"ve_{k}_done") for k in KINDS}
        rs_done = {k: sem(f"rs_{k}_done") for k in KINDS}
        nmr_done = {k: sem(f"nmr_{k}_done") for k in KINDS}
        norm_done = {k: sem(f"norm_{k}_done") for k in ("head", "mid", "fin")}
        emb_done, emb_turned, emb_hi_done, emb_lo_done = sem("emb_done"), sem("emb_turned"), sem("emb_hi_done"), sem("emb_lo_done")
        k_done, kmax_done, kshift_done, kbias_done = sem("k_done"), sem("kmax_done"), sem("kshift_done"), sem("kbias_done")
        ek_done, v_done, q_done, val_done, tanh_q_done, gate_q_done = (sem("ek_done"), sem("v_done"), sem("q_done"),
                                                                     sem("val_done"), sem("tanh_q_done"), sem("gate_q_done"))
        ek_turned, ek_hi_done, ek_lo_done = sem("ek_turned"), sem("ek_hi_done"), sem("ek_lo_done")
        ev_done, ev_hi_done, ev_lo_done = sem("ev_done"), sem("ev_hi_done"), sem("ev_lo_done")
        den_done, num_done, recip_done, ratio_done = sem("den_done"), sem("num_done"), sem("recip_done"), sem("ratio_done")
        y_done, y_hi_done, y_lo_done = sem("y_done"), sem("y_hi_done"), sem("y_lo_done")
        wo_done, res_done, mid_turned = sem("wo_done"), sem("res_done"), sem("mid_turned")
        a_done, a_hi_done, a_lo_done = sem("a_done"), sem("a_hi_done"), sem("a_lo_done")
        w1_done, relu_dve_done, relu_act_done = sem("w1_done"), sem("relu_dve_done"), sem("relu_act_done")
        hid_hi_done, hid_lo_done, w2_done = sem("hid_hi_done"), sem("hid_lo_done"), sem("w2_done")
        x_beta_done, scaled_done, x1_done = sem("x_beta_done"), sem("scaled_done"), sem("x1_done")
        fin_turned, xn_t_done, delta_done = sem("fin_turned"), sem("xn_t_done"), sem("delta_done")
        xk_done, xr_done = sem("xk_done"), sem("xr_done")
        xk_hi_done, xk_lo_done, xr_hi_done, xr_lo_done = sem("xk_hi_done"), sem("xk_lo_done"), sem("xr_hi_done"), sem("xr_lo_done")
        fk_done, fr_done, fv_done = sem("fk_done"), sem("fr_done"), sem("fv_done")
        relu_k_done, sq_done, sq_hi_done, sq_lo_done, tanh_r_done = (sem("relu_k_done"), sem("sq_done"), sem("sq_hi_done"),
                                                                   sem("sq_lo_done"), sem("tanh_r_done"))
        gated_done, out_done = sem("gated_done"), sem("out_done")

        def after(eng, s, count):
            if not isinstance(count, int) or count > 0:
                eng.wait_ge(s, count)

        def most(count, top):
            return min(count, top) if isinstance(count, int) else count

        def f32(ap):
            return ap.bitcast(F32)

        def tile(ap, a, n=D):
            return ap[:, a * n:(a + 1) * n]

        def run_steps(eng, step):
            step(0, 0)
            step(1, 1)
            with eng.Fori(1, 3) as i:
                step(2 * i, 0)
                step(2 * i + 1, 1)
            step(BATCH - 2, 0)
            step(BATCH - 1, 1)

        HP = [2, 1, 0, 2]
        block = ctx.enter_context(nc.Block())

        def rows_of(a, n):
            return a.rearrange("b (a p) d -> p b a d", p=P)[:, bass.ds(n, 1)]

        UNITS = [((A_wk, 0), (A_wq, 0)), ((A_wv, 0), (A_wo, 0)), None, None, None, None,
                 ((A_fk, 0), (A_fr, 0)), ((A_fv, 0),)]

        def load_unit(eng, u):
            dst = stage[UNIT_STAGE[u]]
            if UNITS[u] is not None:
                for k, (a, _) in enumerate(UNITS[u]):
                    eng.dma_start(dst[:, 512 * k:512 * (k + 1)].rearrange("p (c n) -> p c n", c=DC),
                                  a.rearrange("(c p) n -> p c n", p=P)).then_inc(unit_landed[u], 16)
            elif u < 4:
                eng.dma_start(dst, A_w1[(u - 2) * P:(u - 1) * P, :]).then_inc(unit_landed[u], 16)
            else:
                eng.dma_start(dst.rearrange("p (c n) -> p c n", c=4),
                              A_w2.rearrange("(c p) n -> p c n", p=P)[:, 4 * (u - 4):4 * (u - 3)]
                              ).then_inc(unit_landed[u], 16)

        def unit_count(u):
            return 16 * (len(UNITS[u]) if UNITS[u] is not None else 1)

        @block.sync
        def _(sp):
            def load_x(n, p):
                if isinstance(n, int) and n < 2:
                    after(sp, x_landed, 32 * n)
                else:
                    sp.wait_ge(res_done, n - 1)
                sp.dma_start(x_in[p].rearrange("p (b a d) -> p b a d", b=1, a=TT), rows_of(A_x, n)).then_inc(x_landed, 16)
                sp.dma_start(emb[p].rearrange("p (b a d) -> p b a d", b=1, a=TT), rows_of(A_ctx, n)).then_inc(x_landed, 16)

            def store(n):
                sp.wait_ge(out_done, n + 1)
                sp.dma_start(rows_of(out, n), out_sb.rearrange("p (b a d) -> p b a d", b=1, a=TT)).then_inc(out_stored, 16)

            load_x(0, 0)
            sp.dma_start(vec, A_vec).then_inc(vec_landed, 16)
            load_unit(sp, 0)
            load_x(1, 1)
            sp.wait_ge(w_lo_done, 1)
            load_unit(sp, 2)
            sp.wait_ge(pos_turned, 2)
            load_unit(sp, 4)
            sp.wait_ge(w_lo_done, 5)
            load_unit(sp, 6)

            def step(i, p):
                if not (isinstance(i, int) and i == 0):
                    store(i - 1)
                if not isinstance(i, int) or i + 2 < BATCH:
                    load_x(i + 2, p)

            run_steps(sp, step)
            store(BATCH - 1)
            sp.wait_ge(out_stored, 16 * BATCH)

        @block.gpsimd
        def _(pool):
            def stats(kind, n):
                mvs = mv[kind].rearrange("p (a s) -> p s a", s=2)
                pool.wait_ge(mv_done[kind], TT * (n + 1))
                after(pool, nmr_done[kind], n)
                pool.tensor_tensor(ve[kind], mvs[:, 1], eps_col, ALU.add).then_inc(ve_done[kind], 1)
                pool.tensor_tensor(nm[kind], mvs[:, 0], minus_one, ALU.mult).then_inc(ve_done[kind], 1)
                pool.wait_ge(ve_done[kind], 2 * (n + 1))
                if kind == "ff":
                    after(pool, x1_done, TT * n)
                else:
                    after(pool, norm_done[kind], TT * n)
                pool.tensor_tensor(rs[kind], ve[kind], minus_half, ALU.pow).then_inc(rs_done[kind], 1)
                pool.wait_ge(rs_done[kind], n + 1)
                pool.tensor_tensor(nmr[kind], nm[kind], rs[kind], ALU.mult).then_inc(nmr_done[kind], 1)

            def low(dst, src, hi, done):
                pool.tensor_tensor(dst, src, f32(hi), ALU.subtract).then_inc(done, 1)

            def make_emb(n, p):
                pool.wait_ge(x_landed, 32 * (n + 1))
                pool.wait_ge(norm_done["head"], TT * (n + 1))
                pool.tensor_tensor(emb[p], norm, emb[p], ALU.add).then_inc(emb_done, 1)

            def ev_low(n):
                pool.wait_ge(ev_hi_done, n + 1)
                after(pool, num_done, DC * n)
                low(ev_lo, val, ev_hi, ev_lo_done)

            pool.memset(ident, 0.0).then_inc(ident_set, 1)
            pool.wait_ge(ident_set, 1)
            pool.affine_select(out=ident, in_=ident, compare_op=ALU.not_equal, fill=1.0, base=0,
                               pattern=[[-1, P]], channel_multiplier=1).then_inc(ident_set, 1)
            pool.memset(minus_half, -0.5).then_inc(ident_set, 1)
            pool.memset(minus_one, -1.0).then_inc(ident_set, 1)
            pool.memset(eps_col, EPS).then_inc(ident_set, 1)
            pool.wait_ge(ident_set, 5)
            stats("head", 0)
            make_emb(0, 0)
            for u in range(2):
                v = stage[2 + u].rearrange("p (a j) -> p a j", a=2)
                pool.wait_ge(pos_landed[u], 16)
                pool.affine_select(out=v, in_=v, compare_op=ALU.is_gt, fill=0.0, base=BAND + 2 * u * P,
                                   pattern=[[P, 2], [-1, T]], channel_multiplier=1).then_inc(pos_masked, 1)
                pool.wait_ge(pos_masked, 2 * u + 1)
                pool.affine_select(out=v, in_=v, compare_op=ALU.is_gt, fill=0.0, base=BAND - 2 * u * P,
                                   pattern=[[-P, 2], [1, T]], channel_multiplier=-1).then_inc(pos_masked, 1)
            ev_low(0)
            stats("head", 1)
            make_emb(1, 1)

            def step(i, p):
                b, d = i - 1, i + 1
                if not (isinstance(i, int) and i == 0):
                    stats("ff", b)
                    stats("fin", b)
                pool.wait_ge(dve_const, 2)
                pool.wait_ge(x_landed, 32 * (i + 1))
                after(pool, x1_done, TT * i)
                xv = x_in[p].rearrange("p (a d) -> p a d", a=TT)
                bv = beta_t.rearrange("p (o d) -> p o d", o=1).to_broadcast([P, TT, D])
                pool.tensor_tensor(x_beta.rearrange("p (a d) -> p a d", a=TT), xv, bv, ALU.add).then_inc(x_beta_done, 1)
                if not (isinstance(i, int) and i == 0):
                    delta_of(b)
                    pool.wait_ge(xk_hi_done, b + 1)
                    low(xk_lo, xk, xk_hi, xk_lo_done)
                    pool.wait_ge(xr_hi_done, b + 1)
                    low(xr_lo, xr, xr_hi, xr_lo_done)
                pool.wait_ge(y_hi_done, i + 1)
                low(ya_lo, y, ya_hi, y_lo_done)
                if not (isinstance(i, int) and i == 0):
                    pool.wait_ge(sq_hi_done, b + 1)
                    low(xk_lo, xk, xk_hi, sq_lo_done)
                stats("mid", i)
                pool.wait_ge(a_hi_done, i + 1)
                low(ya_lo, res, ya_hi, a_lo_done)
                for q in range(NQ):
                    pool.wait_ge(hid_hi_done, NQ * i + q + 1)
                    low(hid_lo[q % 2], hid[q % 2], hid_hi[q % 2], hid_lo_done)
                    if q == 0 and (not isinstance(i, int) or d < BATCH):
                        ev_low(d)
                if not isinstance(i, int) or i + 2 < BATCH:
                    stats("head", i + 2)
                    make_emb(i + 2, p)

            def delta_of(n):
                pool.wait_ge(xn_t_done, n + 1)
                xv = xn_t.rearrange("p (c t) -> p c t", c=DC)
                pool.tensor_tensor(delta.rearrange("p (c t) -> p c t", c=DC), xv[:, :, 1:T + 1], xv[:, :, 0:T],
                                   ALU.subtract).then_inc(delta_done, 1)

            run_steps(pool, step)
            last = BATCH - 1
            stats("ff", last)
            stats("fin", last)
            delta_of(last)
            pool.wait_ge(xk_hi_done, last + 1)
            low(xk_lo, xk, xk_hi, xk_lo_done)
            pool.wait_ge(xr_hi_done, last + 1)
            low(xr_lo, xr, xr_hi, xr_lo_done)
            pool.wait_ge(sq_hi_done, last + 1)
            low(xk_lo, xk, xk_hi, sq_lo_done)

        @block.vector
        def _(dve):
            def row_stats(kind, n, src):
                after(dve, mv_done[kind], TT * n)
                for a in range(TT):
                    dve.bn_stats(tile(st[kind], a, HD), tile(src, a)).then_inc(st_done[kind], 1)
                dve.wait_ge(st_done[kind], TT * (n + 1))
                after(dve, ve_done[kind], 2 * n)
                if kind == "ff":
                    after(dve, scaled_done, TT * n)
                dve.memset(held, 0.0)
                for a in range(TT):
                    dve.bn_aggr(tile(mv[kind], a, 2), tile(st[kind], a, HD)).then_inc(mv_done[kind], 1)

            def head_stats(n, p):
                dve.wait_ge(x_landed, 32 * (n + 1))
                row_stats("head", n, x_in[p])

            def emb_low(n):
                dve.wait_ge(emb_hi_done, n + 1)
                dve.tensor_tensor(emb_lo, pair(2), f32(emb_hi), ALU.subtract).then_inc(emb_lo_done, 1)

            def key_max(n):
                dve.wait_ge(k_done, n + 1)
                after(dve, kshift_done, n)
                dve.tensor_reduce(kmax, pair(3).rearrange("p (c t) -> p c t", c=DC), AX_X, ALU.max).then_inc(kmax_done, 1)
                dve.wait_ge(kmax_done, n + 1)
                after(dve, kbias_done, n)
                dve.tensor_tensor(kshift, kmax, vec[:, C_BK:C_BK + DC], ALU.add).then_inc(kshift_done, 1)
                dve.wait_ge(kshift_done, n + 1)
                after(dve, ek_done, DC * n)
                dve.tensor_tensor(kbias, vec[:, C_BK:C_BK + DC], kshift, ALU.subtract).then_inc(kbias_done, 1)

            def key_parts(n):
                dve.wait_ge(ek_hi_done, n + 1)
                dve.tensor_tensor(ek_lo, pair(0), f32(ek_hi), ALU.subtract).then_inc(ek_lo_done, 1)
                dve.wait_ge(val_done, n + 1)
                dve.tensor_tensor(val, pair(0), val, ALU.mult).then_inc(ev_done, 1)

            def unit_low(u):
                dve.wait_ge(w_hi_done, u + 1)
                n = unit_cols[u]
                dve.tensor_tensor(w_lo[u][:, :n], stage[UNIT_STAGE[u]][:, :n], f32(w_hi[u])[:, :n],
                                  ALU.subtract).then_inc(w_lo_done, 1)

            def recip(n, c):
                dve.wait_ge(den_done, DC * n + c + 1)
                after(dve, y_lo_done, n)
                dve.reciprocal(tile(y, c, T), bank(0, c)).then_inc(recip_done, 1)

            def make_y(n):
                for c in range(DC):
                    dve.wait_ge(num_done, DC * n + c + 1)
                    dve.wait_ge(recip_done, DC * n + c + 1)
                    dve.tensor_tensor(tile(y, c, T), bank(1, c), tile(y, c, T), ALU.mult).then_inc(ratio_done, 1)
                dve.wait_ge(gate_q_done, n + 1)
                for c in range(DC):
                    dve.wait_ge(ratio_done, DC * n + c + 1)
                    dve.scalar_tensor_tensor(out=tile(y, c, T), in0=tile(y, c, T), scalar=vec[:, C_BV + c:C_BV + c + 1],
                                             in1=tile(gate_q, c, T), op0=ALU.add, op1=ALU.mult).then_inc(y_done, 1)

            def tail_x1(n):
                dve.wait_ge(rs_done["ff"], n + 1)
                after(dve, out_done, n)
                for a in range(TT):
                    dve.scalar_tensor_tensor(out=tile(x1, a), in0=tile(pair(3), a), scalar=mv["ff"][:, 2 * a:2 * a + 1],
                                             in1=gamma_t, op0=ALU.subtract, op1=ALU.mult).then_inc(scaled_done, 1)
                dve.wait_ge(x_beta_done, n + 1)
                for a in range(TT):
                    dve.wait_ge(scaled_done, TT * n + a + 1)
                    dve.scalar_tensor_tensor(out=tile(x1, a), in0=tile(x1, a), scalar=rs["ff"][:, a:a + 1],
                                             in1=tile(x_beta, a), op0=ALU.mult, op1=ALU.add).then_inc(x1_done, 1)

            def tail_stats(n):
                dve.wait_ge(w2_done, NQ * (n + 1))
                row_stats("ff", n, pair(3))

            def fin_stats(n):
                dve.wait_ge(x1_done, TT * (n + 1))
                row_stats("fin", n, x1)

            def mixed(n, dst, mu, done):
                dve.wait_ge(delta_done, n + 1)
                for c in range(DC):
                    dve.scalar_tensor_tensor(out=tile(dst, c, T), in0=tile(delta, c, T), scalar=vec[:, mu + c:mu + c + 1],
                                             in1=xn_t[:, c * (T + 1):c * (T + 1) + T], op0=ALU.mult, op1=ALU.add
                                             ).then_inc(done, 1)

            def mix_inputs(n):
                after(dve, sq_lo_done, n)
                mixed(n, xk, C_MUK, xk_done)
                after(dve, gated_done, n)
                mixed(n, xr, C_MUR, xr_done)

            def square(n):
                dve.wait_ge(relu_k_done, n + 1)
                dve.tensor_tensor(xk, xk, pair(0), ALU.mult).then_inc(sq_done, 1)

            def finish(n):
                dve.wait_ge(fv_done, n + 1)
                dve.wait_ge(tanh_r_done, n + 1)
                after(dve, out_stored, 16 * n)
                dve.scalar_tensor_tensor(out=out_sb, in0=xr, scalar=1.0, in1=pair(0), op0=ALU.add, op1=ALU.mult
                                         ).then_inc(gated_done, 1)
                dve.wait_ge(gated_done, n + 1)
                dve.scalar_tensor_tensor(out=out_sb, in0=out_sb, scalar=gates[:, 1:2], in1=x1, op0=ALU.mult, op1=ALU.add
                                         ).then_inc(out_done, 1)

            dve.memset(f32(ones_r), 1.0).then_inc(const_set, 1)
            dve.memset(f32(bias_r), 0.0).then_inc(const_set, 1)
            dve.memset(xn_t[:, 0:1], 0.0).then_inc(const_set, 1)
            dve.memset(xn_t[:, T + 1:T + 2], 0.0).then_inc(const_set, 1)
            head_stats(0, 0)
            unit_low(0)
            emb_low(0)
            unit_low(1)
            for u in range(2):
                dve.wait_ge(pos_masked, 2 * u + 2)
                dve.tensor_reduce(pos_nmax[:, 2 * u:2 * u + 2], stage[2 + u].rearrange("p (a j) -> p a j", a=2), AX_X,
                                  ALU.max, negate=True).then_inc(pos_max_done, 1)
            key_max(0)
            for u in range(2):
                dve.wait_ge(ew_hi_done, u + 1)
                dve.tensor_tensor(tile(ew_lo, u, PAIR), pair(u), f32(tile(ew_hi, u, PAIR)), ALU.subtract).then_inc(ew_lo_done, 1)
            key_parts(0)
            head_stats(1, 1)
            dve.wait_ge(act_const, 2)
            dve.wait_ge(rows_landed, 48)
            dve.tensor_scalar(gamma_t, gamma_t, gates[:, 0:1], None, ALU.mult).then_inc(dve_const, 1)
            dve.tensor_scalar(beta_t, beta_t, gates[:, 0:1], None, ALU.mult).then_inc(dve_const, 1)
            dve.wait_ge(act_const, 5)
            dve.tensor_scalar(gates[:, 1:2], gates[:, 2:3], 0.5, None, ALU.mult).then_inc(dve_const, 1)
            dve.tensor_tensor(bias_r[32:33, :], bias_f[0:1, :], f32(bias_r)[0:1, :], ALU.subtract).then_inc(dve_const, 1)

            def step(i, p):
                b, d = i - 1, i + 1
                tail = not (isinstance(i, int) and i == 0)
                head = not isinstance(i, int) or d < BATCH
                if tail:
                    tail_stats(b)
                recip(i, 0)
                if tail:
                    tail_x1(b)
                    fin_stats(b)
                recip(i, 1)
                if head:
                    emb_low(d)
                make_y(i)
                if head:
                    key_max(d)
                if tail:
                    mix_inputs(b)
                    square(b)
                else:
                    for u in range(2, 6):
                        unit_low(u)
                dve.wait_ge(wo_done, i + 1)
                after(dve, a_lo_done, i)
                dve.tensor_tensor(res, pair(1), emb[p], ALU.add).then_inc(res_done, 1)
                dve.wait_ge(res_done, i + 1)
                row_stats("mid", i, res)
                if tail:
                    finish(b)
                dve.wait_ge(mid_turned, i + 1)
                for c in range(DC):
                    dve.tensor_scalar(tile(res, c, T), bank(1, c), vec[:, C_GAMMA + c:C_GAMMA + c + 1],
                                      vec[:, C_BETA + c:C_BETA + c + 1], ALU.mult, ALU.add).then_inc(a_done, 1)
                if head:
                    key_parts(d)
                for q in range(NQ):
                    dve.wait_ge(w1_done, NQ * i + q + 1)
                    after(dve, hid_lo_done, NQ * i + q - 1)
                    dve.tensor_scalar(hid[q % 2][:, 0:512], bank(HP[q], 0), vec[:, C_B1 + 2 * q:C_B1 + 2 * q + 1], 0.0,
                                      ALU.add, ALU.max).then_inc(relu_dve_done, 1)
                if not tail:
                    unit_low(6)
                    unit_low(7)
                if not isinstance(i, int) or i + 2 < BATCH:
                    head_stats(i + 2, p)

            run_steps(dve, step)
            last = BATCH - 1
            tail_stats(last)
            tail_x1(last)
            fin_stats(last)
            mix_inputs(last)
            square(last)
            finish(last)

        @block.scalar
        def _(act):
            def normalise(kind, n, src):
                act.wait_ge(nmr_done[kind], n + 1)
                for a in range(TT):
                    act.activation(tile(norm, a), tile(src, a), ACT.Identity, bias=nmr[kind][:, a:a + 1],
                                   scale=rs[kind][:, a:a + 1]).then_inc(norm_done[kind], 1)

            def unit_high(u):
                act.wait_ge(unit_landed[u], unit_count(u))
                n = unit_cols[u]
                act.activation(w_hi[u][:, :n], stage[UNIT_STAGE[u]][:, :n], ACT.Copy).then_inc(w_hi_done, 1)

            def emb_high(n):
                act.wait_ge(emb_turned, n + 1)
                act.activation(emb_hi, pair(2), ACT.Copy).then_inc(emb_hi_done, 1)

            def exp_keys(n):
                act.wait_ge(kbias_done, n + 1)
                after(act, ek_turned, n)
                for c in range(DC):
                    act.activation(tile(ek_t, c, T), bank(3, c), ACT.Exp, bias=kbias[:, c:c + 1]).then_inc(ek_done, 1)

            def keep_values(n):
                act.wait_ge(v_done, n + 1)
                after(act, ev_lo_done, n)
                act.activation(val, pair(3), ACT.Copy).then_inc(val_done, 1)

            def tanh_q(n):
                act.wait_ge(q_done, n + 1)
                after(act, y_done, DC * n)
                for c in range(DC):
                    act.activation(tile(gate_q, c, T), bank(2, c), ACT.Tanh, bias=half_bq[:, c:c + 1], scale=0.5
                                   ).then_inc(tanh_q_done, 1)
                act.wait_ge(tanh_q_done, DC * (n + 1))
                act.activation(gate_q, gate_q, ACT.Copy, bias=0.5, scale=0.5).then_inc(gate_q_done, 1)

            def ek_high(n):
                act.wait_ge(ek_turned, n + 1)
                after(act, num_done, DC * n)
                act.activation(ek_hi, pair(0), ACT.Copy).then_inc(ek_hi_done, 1)

            def ev_high(n):
                act.wait_ge(ev_done, n + 1)
                act.activation(ev_hi, val, ACT.Copy).then_inc(ev_hi_done, 1)

            def fin_norm(n):
                after(act, emb_done, most(n + 2, BATCH))
                after(act, mid_turned, n + 1)
                normalise("fin", n, x1)

            def turned_copy(n):
                act.wait_ge(fin_turned, n + 1)
                after(act, xr_done, DC * n)
                act.activation(xn_t.rearrange("p (c t) -> p c t", c=DC)[:, :, 1:T + 1],
                               pair(2).rearrange("p (c t) -> p c t", c=DC), ACT.Copy).then_inc(xn_t_done, 1)

            def mixed_high(n):
                act.wait_ge(xk_done, DC * (n + 1))
                act.activation(xk_hi, xk, ACT.Copy).then_inc(xk_hi_done, 1)
                act.wait_ge(xr_done, DC * (n + 1))
                act.activation(xr_hi, xr, ACT.Copy).then_inc(xr_hi_done, 1)

            def relu_k(n):
                act.wait_ge(fk_done, n + 1)
                act.activation(xk, pair(0), ACT.Relu).then_inc(relu_k_done, 1)

            def tanh_r(n):
                act.wait_ge(fr_done, n + 1)
                act.activation(xr, pair(2), ACT.Tanh, scale=0.5).then_inc(tanh_r_done, 1)

            def square_high(n):
                act.wait_ge(sq_done, n + 1)
                act.activation(xk_hi, xk, ACT.Copy).then_inc(sq_hi_done, 1)

            act.dma_start(stage[2].rearrange("p (a j) -> p a j", a=2),
                          A_pos.rearrange("(a p) j -> p a j", p=P)[:, 0:2]).then_inc(pos_landed[0], 16)
            act.dma_start(stage[3].rearrange("p (a j) -> p a j", a=2),
                          A_pos.rearrange("(a p) j -> p a j", p=P)[:, 2:4]).then_inc(pos_landed[1], 16)
            load_unit(act, 1)
            act.dma_start(gamma_t, A_rows[:, 0:D]).then_inc(rows_landed, 16)
            act.dma_start(beta_t, A_rows[:, D:2 * D]).then_inc(rows_landed, 16)
            act.dma_start(bias_f[0:1, :], A_bias).then_inc(rows_landed, 16)
            normalise("head", 0, x_in[0])
            unit_high(0)
            emb_high(0)
            unit_high(1)
            act.wait_ge(vec_landed, 16)
            act.activation(half_bq, vec[:, C_BQ:C_BQ + DC], ACT.Copy, scale=0.5).then_inc(act_const, 1)
            act.activation(gates[:, 0:1], vec[:, C_GX:C_GX + 1], ACT.Tanh).then_inc(act_const, 1)
            act.activation(gates[:, 2:3], vec[:, C_GF:C_GF + 1], ACT.Tanh).then_inc(act_const, 1)
            act.wait_ge(ident_set, 2)
            act.activation(ident_r, ident, ACT.Copy).then_inc(act_const, 1)
            act.wait_ge(rows_landed, 48)
            act.wait_ge(const_set, 2)
            act.activation(bias_r[0:1, :], bias_f[0:1, :], ACT.Copy).then_inc(act_const, 1)
            for u in range(2):
                act.wait_ge(pos_max_done, u + 1)
                for a in range(2):
                    v = tile(stage[2 + u], a, T)
                    act.activation(v, v, ACT.Exp, bias=pos_nmax[:, 2 * u + a:2 * u + a + 1]).then_inc(pos_exp_done, 1)
            exp_keys(0)
            keep_values(0)
            act.wait_ge(act_const, 1)
            tanh_q(0)
            for u in range(2):
                act.wait_ge(pos_turned, 2)
                act.activation(tile(ew_hi, u, PAIR), pair(u), ACT.Copy).then_inc(ew_hi_done, 1)
            ek_high(0)
            ev_high(0)
            after(act, emb_done, 1)
            normalise("head", 1, x_in[1])
            act.wait_ge(w_lo_done, 2)
            load_unit(act, 3)
            load_unit(act, 5)

            def step(i, p):
                b, d = i - 1, i + 1
                tail = not (isinstance(i, int) and i == 0)
                head = not isinstance(i, int) or d < BATCH
                if head:
                    if tail:
                        after(act, q_done, d)
                    emb_high(d)
                if tail:
                    fin_norm(b)
                    turned_copy(b)
                if head:
                    exp_keys(d)
                if tail:
                    mixed_high(b)
                act.wait_ge(y_done, DC * (i + 1))
                act.activation(ya_hi, y, ACT.Copy).then_inc(y_hi_done, 1)
                if tail:
                    relu_k(b)
                    tanh_r(b)
                    square_high(b)
                else:
                    for u in range(2, 6):
                        unit_high(u)
                    act.wait_ge(w_lo_done, 6)
                    load_unit(act, 7)
                if head:
                    keep_values(d)
                after(act, fin_turned, i)
                after(act, emb_done, most(i + 2, BATCH))
                normalise("mid", i, res)
                if head:
                    tanh_q(d)
                act.wait_ge(a_done, DC * (i + 1))
                act.activation(ya_hi, res, ACT.Copy).then_inc(a_hi_done, 1)
                if head:
                    ek_high(d)
                for q in range(NQ):
                    j = NQ * i + q
                    act.wait_ge(w1_done, j + 1)
                    after(act, hid_lo_done, j - 1)
                    act.wait_ge(relu_dve_done, j + 1)
                    if tail and q == 0:
                        act.wait_ge(gated_done, i)
                    act.activation(hid[q % 2][:, 512:PAIR], bank(HP[q], 1), ACT.Relu,
                                   bias=vec[:, C_B1 + 2 * q + 1:C_B1 + 2 * q + 2]).then_inc(relu_act_done, 1)
                    after(act, w2_done, j - 1)
                    act.wait_ge(relu_act_done, j + 1)
                    act.activation(hid_hi[q % 2], hid[q % 2], ACT.Copy).then_inc(hid_hi_done, 1)
                    if q == 0 and head:
                        ev_high(d)
                if not tail:
                    unit_high(6)
                    unit_high(7)
                if not isinstance(i, int) or i + 2 < BATCH:
                    act.wait_ge(mid_turned, i + 1)
                    normalise("head", i + 2, x_in[p])

            run_steps(act, step)
            last = BATCH - 1
            fin_norm(last)
            turned_copy(last)
            mixed_high(last)
            relu_k(last)
            tanh_r(last)
            square_high(last)

        @block.tensor
        def _(pe):
            def mm(o, s, m, start, stop):
                return pe.matmul(o, s, m, start=start, stop=stop, skip_group_check=True)

            def turn(dst, src, step_, done):
                for c in range(DC):
                    for a in range(TT):
                        last = pe.transpose(bank(dst, c)[:, a * P:(a + 1) * P],
                                            src[:, step_ * a + c * P:step_ * a + (c + 1) * P], ident)
                last.then_inc(done, 1)

            def unit(u, k):
                return w_hi[u][:, 512 * k:512 * (k + 1)], w_lo[u][:, 512 * k:512 * (k + 1)]

            def channels_out(dst, w, act_hi, act_lo, lo_ready, lo_count, done):
                hi, lo = w
                for c in range(DC):
                    for k in range(DC):
                        for r in (hi, lo):
                            mm(bank(dst, c), r[:, D * k + c * P:D * k + (c + 1) * P], tile(act_hi, k, T),
                               k == 0 and r is hi, False)
                pe.wait_ge(lo_ready, lo_count)
                for c in range(DC):
                    for k in range(DC):
                        last = mm(bank(dst, c), hi[:, D * k + c * P:D * k + (c + 1) * P], tile(act_lo, k, T),
                                  False, k == DC - 1)
                last.then_inc(done, 1)

            def rows_out(dst, w, act_hi, act_lo, lo_ready, lo_count, done, bias=None):
                hi, lo = w
                for a in range(TT):
                    o = tile(pair(dst), a)
                    if bias is not None:
                        mm(o, ones_r, bias, a % 2 == 0, False)
                    for k in range(DC):
                        s = act_hi[:, T * k + a * P:T * k + (a + 1) * P]
                        mm(o, s, tile(hi, k), bias is None and a % 2 == 0 and k == 0, False)
                        mm(o, s, tile(lo, k), False, False)
                pe.wait_ge(lo_ready, lo_count)
                for a in range(TT):
                    o = tile(pair(dst), a)
                    for k in range(DC):
                        s = act_lo[:, T * k + a * P:T * k + (a + 1) * P]
                        last = mm(o, s, tile(hi, k), False, a % 2 == 1 and k == DC - 1)
                last.then_inc(done, 1)

            def turn_emb(n, p):
                pe.wait_ge(emb_done, n + 1)
                after(pe, tanh_q_done, DC * n)
                after(pe, relu_act_done, NQ * (n - 1))
                after(pe, relu_dve_done, NQ * (n - 1))
                turn(2, emb[p], D, emb_turned)

            def keys(n):
                pe.wait_ge(emb_hi_done, n + 1)
                after(pe, scaled_done, TT * (n - 1))
                after(pe, val_done, n)
                channels_out(3, unit(0, 0), emb_hi, emb_lo, emb_lo_done, n + 1, k_done)

            def values(n):
                pe.wait_ge(ek_done, DC * (n + 1))
                rows_out(3, unit(1, 0), emb_hi, emb_lo, emb_lo_done, n + 1, v_done)

            def queries(n):
                after(pe, tanh_r_done, n - 1)
                pe.wait_ge(emb_lo_done, n + 1)
                channels_out(2, unit(0, 1), emb_hi, emb_lo, emb_lo_done, n + 1, q_done)

            def turn_keys(n):
                after(pe, recip_done, DC * n)
                after(pe, gated_done, n - 1)
                for a in range(TT):
                    for c in range(DC):
                        last = pe.transpose(tile(pair(0), a)[:, c * P:(c + 1) * P],
                                            ek_t[:, T * c + a * P:T * c + (a + 1) * P], ident)
                last.then_inc(ek_turned, 1)

            def weigh(dst, c, hi, lo, done):
                for j in range(TT):
                    s = slice(D * j + c * P, D * j + (c + 1) * P)
                    mm(bank(dst, c), hi[:, s], tile(ew_hi, j, T), j == 0, False)
                    mm(bank(dst, c), hi[:, s], tile(ew_lo, j, T), False, False)
                    last = mm(bank(dst, c), lo[:, s], tile(ew_hi, j, T), False, j == TT - 1)
                last.then_inc(done, 1)

            def hidden(n, q):
                for b in range(2):
                    m = 2 * q + b
                    for k in range(DC):
                        for w in (w_hi, w_lo):
                            mm(bank(HP[q], b), w[2 + k][:, m * P:(m + 1) * P], tile(ya_hi, k, T), k == 0 and w is w_hi, False)
                pe.wait_ge(a_lo_done, n + 1)
                for b in range(2):
                    m = 2 * q + b
                    for k in range(DC):
                        last = mm(bank(HP[q], b), w_hi[2 + k][:, m * P:(m + 1) * P], tile(ya_lo, k, T), False, k == DC - 1)
                last.then_inc(w1_done, 1)

            def start_ff(n):
                pe.wait_ge(a_lo_done, n + 1)
                for a in range(TT):
                    o = tile(pair(3), a)
                    mm(o, ones_r, bias_r[:, D:2 * D], a % 2 == 0, False)
                    for k in range(DC):
                        for part in (ya_hi, ya_lo):
                            mm(o[:, k * P:(k + 1) * P], part[:, T * k + a * P:T * k + (a + 1) * P], ident_r, False, False)

            def add_hidden(n, q):
                r = q % 2
                pe.wait_ge(hid_hi_done, NQ * n + q + 1)
                for a in range(TT):
                    for b in range(2):
                        m = 2 * q + b
                        w = slice(D * (m % 4), D * (m % 4 + 1))
                        s = hid_hi[r][:, T * b + a * P:T * b + (a + 1) * P]
                        mm(tile(pair(3), a), s, w_hi[4 + m // 4][:, w], False, False)
                        mm(tile(pair(3), a), s, w_lo[4 + m // 4][:, w], False, False)
                pe.wait_ge(hid_lo_done, NQ * n + q + 1)
                for a in range(TT):
                    for b in range(2):
                        m = 2 * q + b
                        w = slice(D * (m % 4), D * (m % 4 + 1))
                        s = hid_lo[r][:, T * b + a * P:T * b + (a + 1) * P]
                        last = mm(tile(pair(3), a), s, w_hi[4 + m // 4][:, w], False, q == NQ - 1 and b == 1 and a % 2 == 1)
                last.then_inc(w2_done, 1)

            def turn_fin(n):
                pe.wait_ge(norm_done["fin"], TT * (n + 1))
                pe.wait_ge(emb_lo_done, most(n + 3, BATCH))
                pe.wait_ge(relu_act_done, NQ * (n + 1))
                pe.wait_ge(relu_dve_done, NQ * (n + 1))
                turn(2, norm, D, fin_turned)

            def ffn_k(n):
                pe.wait_ge(recip_done, most(DC * (n + 2), DC * BATCH))
                pe.wait_ge(xk_hi_done, n + 1)
                channels_out(0, unit(6, 0), xk_hi, xk_lo, xk_lo_done, n + 1, fk_done)

            def ffn_r(n):
                pe.wait_ge(xn_t_done, n + 1)
                pe.wait_ge(xr_hi_done, n + 1)
                rows_out(2, unit(6, 1), xr_hi, xr_lo, xr_lo_done, n + 1, fr_done)

            def ffn_v(n):
                pe.wait_ge(sq_hi_done, n + 1)
                rows_out(0, unit(7, 0), xk_hi, xk_lo, sq_lo_done, n + 1, fv_done)

            pe.wait_ge(ident_set, 2)
            turn_emb(0, 0)
            pe.wait_ge(w_lo_done, 1)
            keys(0)
            pe.wait_ge(w_lo_done, 2)
            values(0)
            queries(0)
            pe.wait_ge(pos_exp_done, TT)
            for u in range(2):
                for b in range(2):
                    for a in range(TT):
                        j = 2 * u + b
                        last = pe.transpose(bank(u, b)[:, a * P:(a + 1) * P],
                                            stage[2 + a // 2][:, T * (a % 2) + j * P:T * (a % 2) + (j + 1) * P], ident)
                last.then_inc(pos_turned, 1)
            pe.wait_ge(ew_lo_done, 1)
            turn_keys(0)

            def step(i, p):
                b, d = i - 1, i + 1
                tail = not (isinstance(i, int) and i == 0)
                head = not isinstance(i, int) or d < BATCH
                pe.wait_ge(ek_lo_done, i + 1)
                pe.wait_ge(ev_done, i + 1)
                if tail:
                    pe.wait_ge(relu_act_done, NQ * i)
                    pe.wait_ge(relu_dve_done, NQ * i)
                else:
                    pe.wait_ge(ew_lo_done, 2)
                for c in range(DC):
                    weigh(0, c, ek_hi, ek_lo, den_done)
                if head:
                    turn_emb(d, 1 - p)
                pe.wait_ge(ev_lo_done, i + 1)
                for c in range(DC):
                    weigh(1, c, ev_hi, ev_lo, num_done)
                if head:
                    keys(d)
                if tail:
                    turn_fin(b)
                    ffn_k(b)
                    ffn_r(b)
                else:
                    pe.wait_ge(act_const, 5)
                    pe.wait_ge(dve_const, 4)
                pe.wait_ge(y_hi_done, i + 1)
                rows_out(1, unit(1, 1), ya_hi, ya_lo, y_lo_done, i + 1, wo_done, bias=bias_r[:, 0:D])
                if head:
                    values(d)
                if tail:
                    ffn_v(b)
                if head:
                    queries(d)
                pe.wait_ge(norm_done["mid"], TT * (i + 1))
                turn(1, norm, D, mid_turned)
                if head:
                    turn_keys(d)
                pe.wait_ge(a_hi_done, i + 1)
                if not tail:
                    pe.wait_ge(w_lo_done, 6)
                if head:
                    pe.wait_ge(tanh_q_done, DC * (d + 1))
                else:
                    pe.wait_ge(tanh_r_done, i)
                hidden(i, 0)
                hidden(i, 1)
                if head:
                    pe.wait_ge(val_done, d + 1)
                start_ff(i)
                add_hidden(i, 0)
                if head:
                    pe.wait_ge(ev_done, d + 1)
                else:
                    pe.wait_ge(gated_done, i)
                hidden(i, 2)
                add_hidden(i, 1)
                pe.wait_ge(relu_act_done, NQ * i + 1)
                pe.wait_ge(relu_dve_done, NQ * i + 1)
                hidden(i, 3)
                add_hidden(i, 2)
                add_hidden(i, 3)

            run_steps(pe, step)
            last = BATCH - 1
            turn_fin(last)
            ffn_k(last)
            ffn_r(last)
            ffn_v(last)


_SHAPE = (BATCH, T, D)


def kernel(x, ctx_1024, g_xattn, g_ffn, L0_xattn_wq, L0_xattn_bq, L0_xattn_wk, L0_xattn_bk, L0_xattn_wv, L0_xattn_bv,
           L0_xattn_wo, L0_xattn_bo, L0_xattn_pos_bias, L0_xattn_gamma, L0_xattn_beta, L0_xattn_w1, L0_xattn_b1,
           L0_xattn_w2, L0_xattn_b2, L0_ffn_W_r, L0_ffn_W_k, L0_ffn_W_v, L0_ffn_mu_r, L0_ffn_mu_k):
    import numpy as np
    import concourse.bacc as bacc
    from concourse.bass_utils import run_bass_kernel_spmd

    def columns(v):
        return np.asarray(v).reshape(-1, P).T

    vec = np.concatenate([columns(v) for v in (L0_xattn_bq, L0_xattn_bk, L0_xattn_bv, L0_xattn_gamma, L0_xattn_beta,
                                               L0_ffn_mu_r, L0_ffn_mu_k, L0_xattn_b1)]
                         + [np.broadcast_to(np.asarray(g).reshape(1, 1), (P, 1)) for g in (g_xattn, g_ffn)], axis=1)
    rows = np.broadcast_to(np.concatenate([np.asarray(L0_xattn_gamma), np.asarray(L0_xattn_beta)])[None, :], (P, 2 * D))
    bias = np.concatenate([np.asarray(L0_xattn_bo), np.asarray(L0_xattn_b2)])[None, :]
    named = {
        "x": x, "ctx": ctx_1024, "vec": vec, "rows": rows, "bias": bias, "pos": L0_xattn_pos_bias,
        "wk": L0_xattn_wk, "wq": L0_xattn_wq, "wv": L0_xattn_wv, "wo": L0_xattn_wo, "w1": L0_xattn_w1, "w2": L0_xattn_w2,
        "fk": np.asarray(L0_ffn_W_k).T, "fr": np.asarray(L0_ffn_W_r).T, "fv": np.asarray(L0_ffn_W_v).T,
    }
    nc = bacc.Bacc("TRN2", target_bir_lowering=False, num_devices=1)
    arrays, args = {}, []
    for name, a in named.items():
        a = np.ascontiguousarray(a)
        arrays[f"in_{name}"] = a
        args.append(nc.dram_tensor(f"in_{name}", a.shape, mybir.dt.from_np(a.dtype), kind="ExternalInput").ap())
    args.append(nc.dram_tensor("out_0", _SHAPE, F32, kind="ExternalOutput").ap())
    flamingo_gated_block(nc, *args)
    r = run_bass_kernel_spmd(nc, [arrays], core_ids=[0])
    return r.results[0]["out_0"]
```

```python
from contextlib import ExitStack

import concourse.bass as bass
from concourse import mybir

F32 = mybir.dt.float32
F32R = mybir.dt.float32r
ALU = mybir.AluOpType
ACT = mybir.ActivationFunctionType
AX_X = mybir.AxisListType.X

P = 128
BATCH = 8
T = 512
D = 256
H = 1024
BAND = 64
EPS = 1e-5
TT = T // P
DC = D // P
HC = H // P
NQ = HC // 2
PAIR = 1024
HD = 6
WIN = 2 * P
FAR = 64 + TT
FIN_DVE = 3
FIRST_DVE = 2
NU = 8

C_BQ, C_BK, C_BV, C_GAMMA, C_BETA, C_MUR, C_MUK, C_B2, C_B1 = range(0, 9 * DC, DC)
C_GX = C_B1 + HC
C_GF = C_GX + 1
NVEC = C_GF + 1


def window(j):
    return min(max(j * P - BAND, 0), T - WIN)


def flamingo_gated_block(nc, A_x, A_ctx, A_vec, A_rows, A_far, A_pos, A_wk, A_wq, A_wv, A_wo,
                         A_w1, A_w2, A_fk, A_fr, A_fv, out):
    ctx = ExitStack()
    with ctx:
        def sb(name, cols, dt=F32):
            return ctx.enter_context(nc.sbuf_tensor(name, [P, cols], dt))[:, :]

        def sem(name):
            return ctx.enter_context(nc.semaphore(name))

        ident = sb("ident", P)
        vec = sb("vec", NVEC)
        half_bq = sb("half_bq", DC)
        gates = sb("gates", 3)
        gamma_t = sb("gamma_t", D)
        beta_t = sb("beta_t", D)
        bo_rows = sb("bo_rows", D)
        minus_half, minus_one, eps_col = sb("minus_half", TT), sb("minus_one", TT), sb("eps_col", TT)
        unit_cols = [PAIR] * (NU - 1) + [DC * D]
        w_hi = [sb(f"w_hi{u}", unit_cols[u], F32R) for u in range(NU)]
        w_lo = [sb(f"w_lo{u}", unit_cols[u], F32R) for u in range(NU)]
        ew_hi = sb("ew_hi", TT * WIN, F32R)
        ew_lo = sb("ew_lo", TT * WIN, F32R)
        far_in = sb("far_in", 2 * TT * FAR)
        tile_rows = sb("tile_rows", TT * FAR, F32R)
        far_c = sb("far_c", T, F32R)
        c_col = sb("c_col", TT)
        sums, sums_r = sb("sums", D), sb("sums_r", D, F32R)
        pos_nmax = sb("pos_nmax", TT)

        emb = [sb(f"emb{p}", TT * D) for p in range(2)]
        norm = sb("norm", TT * D)
        emb_hi, emb_lo = sb("emb_hi", DC * T, F32R), sb("emb_lo", DC * T, F32R)
        y = sb("y", DC * T)
        ek_t = y
        gate_q = sb("gate_q", DC * T)
        ek_hi, ek_lo = sb("ek_hi", TT * D, F32R), sb("ek_lo", TT * D, F32R)
        y_hi, y_lo = ek_hi, ek_lo
        ev_hi, ev_lo = sb("ev_hi", TT * D, F32R), sb("ev_lo", TT * D, F32R)
        sq_hi, sq_lo = ev_hi, ev_lo
        res = sb("res", TT * D)
        val = res
        a_t = sb("a_t", DC * T)
        a_hi, a_lo = sb("a_hi", DC * T, F32R), sb("a_lo", DC * T, F32R)
        hid = [sb(f"hid{r}", PAIR) for r in range(2)]
        hid_hi = [sb(f"hid_hi{r}", PAIR, F32R) for r in range(2)]
        hid_lo = [sb(f"hid_lo{r}", PAIR, F32R) for r in range(2)]
        x_beta = sb("x_beta", TT * D)
        x1 = sb("x1", TT * D)
        xn_t = sb("xn_t", DC * (T + 1))
        x_in = sb("x_in", TT * D)
        xk = x_in
        xk_hi, xk_lo = sb("xk_hi", DC * T, F32R), sb("xk_lo", DC * T, F32R)
        xr = sb("xr", DC * T)
        xr_hi, xr_lo = hid_hi[0], hid_lo[0]
        out_sb = sb("out_sb", TT * D)
        delta = out_sb
        stage = [hid[0], hid[1], x1, out_sb]
        UNIT_STAGE = [0, 1, 0, 1, 2, 3, 2, 3]

        KINDS = ("head", "mid", "ff", "fin")
        st = {k: sb(f"st_{k}", TT * HD) for k in KINDS}
        mv = {k: sb(f"mv_{k}", TT * 2) for k in KINDS}
        ve = {k: sb(f"ve_{k}", TT) for k in KINDS}
        nm = {k: sb(f"nm_{k}", TT) for k in KINDS}
        rs = {k: sb(f"rs_{k}", TT) for k in KINDS}
        nmr = {k: sb(f"nmr_{k}", TT) for k in KINDS}
        held = sb("held", 1)
        kmax, kshift, kbias = sb("kmax", DC), sb("kshift", DC), sb("kbias", DC)

        ps = ctx.enter_context(nc.psum_tensor("ps", [P, 4 * PAIR], F32))

        def bank(pair, b=0, n=512):
            o = pair * PAIR + 512 * b
            return ps[:, o:o + n]

        def pair(k):
            return ps[:, k * PAIR:(k + 1) * PAIR]

        x_landed, ctx_landed, again_landed, out_stored = sem("x_landed"), sem("ctx_landed"), sem("again_landed"), sem("out_stored")
        vec_landed, rows_landed, far_landed = sem("vec_landed"), sem("rows_landed"), sem("far_landed")
        tile_rows_done, c_col_done, far_masked, far_turned = (sem("tile_rows_done"), sem("c_col_done"),
                                                              sem("far_masked"), sem("far_turned"))
        far_hi_done, far_lo_done = sem("far_hi_done"), sem("far_lo_done")
        sums_done, sums_kept, sums_hi_done, sums_lo_done = (sem("sums_done"), sem("sums_kept"), sem("sums_hi_done"),
                                                            sem("sums_lo_done"))
        unit_landed = [sem(f"unit_landed{u}") for u in range(NU)]
        pos_landed = [sem(f"pos_landed{u}") for u in range(2)]
        ident_set, const_set, dve_const, act_const = sem("ident_set"), sem("const_set"), sem("dve_const"), sem("act_const")
        w_hi_done, w_lo_done = sem("w_hi_done"), sem("w_lo_done")
        pos_masked, pos_max_done, pos_exp_done = sem("pos_masked"), sem("pos_max_done"), sem("pos_exp_done")
        pos_turned, ew_hi_done, ew_lo_done = sem("pos_turned"), sem("ew_hi_done"), sem("ew_lo_done")
        st_done = {k: sem(f"st_{k}_done") for k in KINDS}
        mv_done = {k: sem(f"mv_{k}_done") for k in KINDS}
        ve_done = {k: sem(f"ve_{k}_done") for k in KINDS}
        rs_done = {k: sem(f"rs_{k}_done") for k in KINDS}
        nmr_done = {k: sem(f"nmr_{k}_done") for k in KINDS}
        norm_done = {k: sem(f"norm_{k}_done") for k in ("head", "mid", "fin")}
        emb_bo_done, ff_sum_done, ff_turned = sem("emb_bo_done"), sem("ff_sum_done"), sem("ff_turned")
        emb_done, emb_turned, emb_hi_done, emb_lo_done = sem("emb_done"), sem("emb_turned"), sem("emb_hi_done"), sem("emb_lo_done")
        k_done, kmax_done, kshift_done, kbias_done = sem("k_done"), sem("kmax_done"), sem("kshift_done"), sem("kbias_done")
        ek_done, v_done, q_done, val_done, tanh_q_done, gate_q_done = (sem("ek_done"), sem("v_done"), sem("q_done"),
                                                                     sem("val_done"), sem("tanh_q_done"), sem("gate_q_done"))
        ek_turned, ek_hi_done, ek_lo_done = sem("ek_turned"), sem("ek_hi_done"), sem("ek_lo_done")
        ev_done, ev_hi_done, ev_lo_done = sem("ev_done"), sem("ev_hi_done"), sem("ev_lo_done")
        den_done, num_done, recip_done, ratio_done = sem("den_done"), sem("num_done"), sem("recip_done"), sem("ratio_done")
        y_done, y_hi_done, y_lo_done = sem("y_done"), sem("y_hi_done"), sem("y_lo_done")
        wo_done, res_done, mid_turned = sem("wo_done"), sem("res_done"), sem("mid_turned")
        a_done, a_hi_done, a_lo_done = sem("a_done"), sem("a_hi_done"), sem("a_lo_done")
        w1_done, relu_dve_done, relu_act_done = sem("w1_done"), sem("relu_dve_done"), sem("relu_act_done")
        hid_hi_done, hid_lo_done, w2_done, ff_half_done = sem("hid_hi_done"), sem("hid_lo_done"), sem("w2_done"), sem("ff_half_done")
        x_beta_done, scaled_done, x1_done = sem("x_beta_done"), sem("scaled_done"), sem("x1_done")
        fin_turned, xn_t_done, delta_done = sem("fin_turned"), sem("xn_t_done"), sem("delta_done")
        xk_done, xr_done = sem("xk_done"), sem("xr_done")
        xk_hi_done, xk_lo_done, xr_hi_done, xr_lo_done = sem("xk_hi_done"), sem("xk_lo_done"), sem("xr_hi_done"), sem("xr_lo_done")
        fk_done, fr_done, fv_done = sem("fk_done"), sem("fr_done"), sem("fv_done")
        relu_k_done, sq_done, sq_hi_done, sq_lo_done, tanh_r_done = (sem("relu_k_done"), sem("sq_done"), sem("sq_hi_done"),
                                                                   sem("sq_lo_done"), sem("tanh_r_done"))
        gated_done, out_done = sem("gated_done"), sem("out_done")

        def after(eng, s, count):
            if not isinstance(count, int) or count > 0:
                eng.wait_ge(s, count)

        def most(count, top):
            return min(count, top) if isinstance(count, int) else count

        def has(n):
            return not isinstance(n, int) or 0 <= n < BATCH

        def f32(ap):
            return ap.bitcast(F32)

        def tile(ap, a, n=D):
            return ap[:, a * n:(a + 1) * n]

        def low(eng, dst, src, hi, ready, count, done):
            eng.wait_ge(ready, count)
            eng.tensor_tensor(dst, src, f32(hi), ALU.subtract).then_inc(done, 1)

        def hidden_low(eng, n, q):
            low(eng, hid_lo[q % 2], hid[q % 2], hid_hi[q % 2], hid_hi_done, NQ * n + q + 1, hid_lo_done)

        def xk_low(eng, n):
            low(eng, xk_lo, xk, xk_hi, xk_hi_done, n + 1, xk_lo_done)

        def xr_low(eng, n):
            low(eng, xr_lo, xr, xr_hi, xr_hi_done, n + 1, xr_lo_done)

        def sq_low(eng, n):
            low(eng, sq_lo, xk, sq_hi, sq_hi_done, n + 1, sq_lo_done)

        def make_emb(eng, n, p):
            eng.wait_ge(ctx_landed, 16 * (n + 1))
            eng.wait_ge(norm_done["head"], TT * (n + 1))
            eng.tensor_tensor(emb[p], norm, emb[p], ALU.add).then_inc(emb_done, 1)

        def delta_of(eng, n):
            eng.wait_ge(xn_t_done, n + 1)
            after(eng, out_stored, 16 * n)
            xv = xn_t.rearrange("p (c t) -> p c t", c=DC)
            eng.tensor_tensor(delta.rearrange("p (c t) -> p c t", c=DC), xv[:, :, 1:T + 1], xv[:, :, 0:T],
                              ALU.subtract).then_inc(delta_done, 1)

        def x1_of(n):
            return emb[BATCH % 2] if isinstance(n, int) and n == BATCH - 1 else x1

        def run_steps(eng, step):
            step(0, 0)
            step(1, 1)
            with eng.Fori(1, 3) as i:
                step(2 * i, 0)
                step(2 * i + 1, 1)
            for n in range(BATCH - 2, BATCH):
                step(n, n % 2)

        def ew_window(j):
            return bank(2 + j // 2, j % 2)[:, window(j):window(j) + WIN]

        HP = [0, 2, 0, 1]
        block = ctx.enter_context(nc.Block())

        def rows_of(a, n):
            return a.rearrange("b (a p) d -> p b a d", p=P)[:, bass.ds(n, 1)]

        UNITS = [((A_wk, 0), (A_wq, 0)), ((A_wv, 0), (A_wo, 0)), None, None, None, None,
                 ((A_fk, 0), (A_fr, 0)), ((A_fv, 0),)]

        def load_unit(eng, u):
            dst = stage[UNIT_STAGE[u]]
            if UNITS[u] is not None:
                for k, (a, _) in enumerate(UNITS[u]):
                    eng.dma_start(dst[:, 512 * k:512 * (k + 1)].rearrange("p (c n) -> p c n", c=DC),
                                  a.rearrange("(c p) n -> p c n", p=P)).then_inc(unit_landed[u], 16)
            elif u < 4:
                eng.dma_start(dst, A_w1[(u - 2) * P:(u - 1) * P, :]).then_inc(unit_landed[u], 16)
            else:
                eng.dma_start(dst.rearrange("p (c n) -> p c n", c=4),
                              A_w2.rearrange("(c p) n -> p c n", p=P)[:, 4 * (u - 4):4 * (u - 3)]
                              ).then_inc(unit_landed[u], 16)

        def unit_count(u):
            return 16 * (len(UNITS[u]) if UNITS[u] is not None else 1)

        @block.sync
        def _(sp):
            def batch_dma(sb_tile, dram, n):
                return sb_tile.rearrange("p (b a d) -> p b a d", b=1, a=TT), rows_of(dram, n)

            def load_x(n):
                if has(n - 4) and not (isinstance(n, int) and n < 4):
                    sp.wait_ge(sq_lo_done, n - 3)
                after(sp, norm_done["head"], TT * n)
                sp.dma_start(*batch_dma(x_in, A_x, n)).then_inc(x_landed, 16)

            def load_ctx(n, p):
                after(sp, res_done, n - 1)
                after(sp, emb_done, n)
                sp.dma_start(*batch_dma(emb[p], A_ctx, n)).then_inc(ctx_landed, 16)

            def load_again(n):
                after(sp, x1_done, TT * n)
                sp.dma_start(*batch_dma(x_beta, A_x, n)).then_inc(again_landed, 16)

            def store(n):
                sp.wait_ge(out_done, n + 1)
                sp.dma_start(rows_of(out, n), out_sb.rearrange("p (b a d) -> p b a d", b=1, a=TT)).then_inc(out_stored, 16)

            load_x(0)
            load_ctx(0, 0)
            load_unit(sp, 0)
            sp.dma_start(vec, A_vec).then_inc(vec_landed, 16)
            sp.dma_start(far_in, A_far).then_inc(far_landed, 16)
            load_x(1)
            load_ctx(1, 1)
            for u in (2, 3):
                sp.wait_ge(w_lo_done, u - 1)
                load_unit(sp, u)
            sp.wait_ge(pos_turned, 2)
            load_unit(sp, 4)
            load_unit(sp, 5)
            for u in (6, 7):
                sp.wait_ge(w_lo_done, u - 1)
                load_unit(sp, u)

            def step(i, p):
                if has(i - 1):
                    load_again(i - 1)
                if has(i + 2):
                    load_x(i + 2)
                    load_ctx(i + 2, p)
                if has(i - 2):
                    store(i - 2)

            run_steps(sp, step)
            load_again(BATCH - 1)
            store(BATCH - 2)
            store(BATCH - 1)
            sp.wait_ge(out_stored, 16 * BATCH)

        @block.gpsimd
        def _(pool):
            def stats(kind, n):
                mvs = mv[kind].rearrange("p (a s) -> p s a", s=2)
                pool.wait_ge(mv_done[kind], TT * (n + 1))
                after(pool, nmr_done[kind], n)
                pool.tensor_tensor(ve[kind], mvs[:, 1], eps_col, ALU.add).then_inc(ve_done[kind], 1)
                pool.tensor_tensor(nm[kind], mvs[:, 0], minus_one, ALU.mult).then_inc(ve_done[kind], 1)
                pool.wait_ge(ve_done[kind], 2 * (n + 1))
                if kind == "ff":
                    after(pool, x1_done, TT * n)
                else:
                    after(pool, norm_done[kind], TT * n)
                pool.tensor_tensor(rs[kind], ve[kind], minus_half, ALU.pow).then_inc(rs_done[kind], 1)
                pool.wait_ge(rs_done[kind], n + 1)
                pool.tensor_tensor(nmr[kind], nm[kind], rs[kind], ALU.mult).then_inc(nmr_done[kind], 1)


            def add_row(ap, row, done):
                v = ap.rearrange("p (a d) -> p a d", a=TT)
                r = row.rearrange("p (o d) -> p o d", o=1).to_broadcast([P, TT, D])
                pool.tensor_tensor(v, v, r, ALU.add).then_inc(done, 1)

            def emb_plus_bo(n, p):
                pool.wait_ge(emb_turned, n + 1)
                pool.wait_ge(rows_landed, 48)
                add_row(emb[p], bo_rows, emb_bo_done)

            def x_plus_beta(n):
                pool.wait_ge(dve_const, 2)
                pool.wait_ge(again_landed, 16 * (n + 1))
                add_row(x_beta, beta_t, x_beta_done)

            def ev_low(n):
                low(pool, ev_lo, val, ev_hi, ev_hi_done, n + 1, ev_lo_done)

            pool.memset(ident, 0.0).then_inc(ident_set, 1)
            pool.wait_ge(ident_set, 1)
            pool.affine_select(out=ident, in_=ident, compare_op=ALU.not_equal, fill=1.0, base=0,
                               pattern=[[-1, P]], channel_multiplier=1).then_inc(ident_set, 1)
            pool.memset(minus_half, -0.5).then_inc(ident_set, 1)
            pool.memset(minus_one, -1.0).then_inc(ident_set, 1)
            pool.memset(eps_col, EPS).then_inc(ident_set, 1)
            pool.wait_ge(ident_set, 5)
            stats("head", 0)
            for u in range(2):
                v = stage[2 + u].rearrange("p (a j) -> p a j", a=2)
                pool.wait_ge(pos_landed[u], 16)
                pool.affine_select(out=v, in_=v, compare_op=ALU.is_gt, fill=0.0, base=BAND + 2 * u * P,
                                   pattern=[[P, 2], [-1, T]], channel_multiplier=1).then_inc(pos_masked, 1)
                pool.wait_ge(pos_masked, 2 * u + 1)
                pool.affine_select(out=v, in_=v, compare_op=ALU.is_gt, fill=0.0, base=BAND - 2 * u * P,
                                   pattern=[[-P, 2], [1, T]], channel_multiplier=-1).then_inc(pos_masked, 1)
            emb_plus_bo(0, 0)
            stats("head", 1)
            make_emb(pool, 1, 1)

            def step(i, p):
                a, b, d, e = i - 2, i - 1, i + 1, i + 2
                ev_low(i)
                if has(a):
                    delta_of(pool, a)
                if has(b):
                    hidden_low(pool, b, 1)
                if has(a):
                    xk_low(pool, a)
                    xr_low(pool, a)
                if has(d):
                    emb_plus_bo(d, 1 - p)
                low(pool, y_lo, y, y_hi, y_hi_done, i + 1, y_lo_done)
                if has(a):
                    sq_low(pool, a)
                if has(b):
                    hidden_low(pool, b, 2)
                stats("mid", i)
                if has(b):
                    hidden_low(pool, b, 3)
                    x_plus_beta(b)
                if has(e):
                    stats("head", e)
                if has(b):
                    stats("ff", b)
                if has(e):
                    make_emb(pool, e, p)
                hidden_low(pool, i, 0)
                if has(b):
                    stats("fin", b)

            run_steps(pool, step)
            a, b = BATCH - 2, BATCH - 1
            hidden_low(pool, b, 1)
            hidden_low(pool, b, 2)
            x_plus_beta(b)
            xr_low(pool, a)
            stats("ff", b)
            sq_low(pool, a)
            stats("fin", b)

        @block.vector
        def _(dve):
            def row_stats(kind, n, src):
                after(dve, mv_done[kind], TT * n)
                for a in range(TT):
                    dve.bn_stats(tile(st[kind], a, HD), tile(src, a)).then_inc(st_done[kind], 1)
                dve.wait_ge(st_done[kind], TT * (n + 1))
                after(dve, ve_done[kind], 2 * n)
                if kind == "ff":
                    after(dve, scaled_done, TT * n)
                dve.memset(held, 0.0)
                for a in range(TT):
                    dve.bn_aggr(tile(mv[kind], a, 2), tile(st[kind], a, HD)).then_inc(mv_done[kind], 1)

            def head_stats(n):
                dve.wait_ge(x_landed, 16 * (n + 1))
                row_stats("head", n, x_in)

            def emb_low(n):
                dve.wait_ge(emb_hi_done, n + 1)
                dve.tensor_tensor(emb_lo, pair(0), f32(emb_hi), ALU.subtract).then_inc(emb_lo_done, 1)

            def key_max(n):
                dve.wait_ge(k_done, n + 1)
                after(dve, kshift_done, n)
                dve.tensor_reduce(kmax, pair(1).rearrange("p (c t) -> p c t", c=DC), AX_X, ALU.max).then_inc(kmax_done, 1)
                dve.wait_ge(kmax_done, n + 1)
                after(dve, kbias_done, n)
                dve.tensor_tensor(kshift, kmax, vec[:, C_BK:C_BK + DC], ALU.add).then_inc(kshift_done, 1)
                dve.wait_ge(kshift_done, n + 1)
                after(dve, ek_done, DC * n)
                dve.tensor_tensor(kbias, vec[:, C_BK:C_BK + DC], kshift, ALU.subtract).then_inc(kbias_done, 1)

            def keep_values(n, src=1):
                dve.wait_ge(v_done, n + 1)
                after(dve, ff_turned, n - 1)
                after(dve, norm_done["mid"], TT * n)
                dve.tensor_copy(val, pair(src)).then_inc(val_done, 1)

            def key_parts(n):
                dve.wait_ge(ek_hi_done, n + 1)
                dve.tensor_tensor(ek_lo, pair(0), f32(ek_hi), ALU.subtract).then_inc(ek_lo_done, 1)
                dve.wait_ge(val_done, n + 1)
                dve.tensor_tensor(val, pair(0), val, ALU.mult).then_inc(ev_done, 1)

            def unit_low(u):
                dve.wait_ge(w_hi_done, u + 1)
                n = unit_cols[u]
                dve.tensor_tensor(w_lo[u][:, :n], stage[UNIT_STAGE[u]][:, :n], f32(w_hi[u])[:, :n],
                                  ALU.subtract).then_inc(w_lo_done, 1)

            def sums_low(n, part):
                dve.wait_ge(sums_hi_done, 2 * n + part + 1)
                src = sums if part == 1 else bank(2, 0, D)
                dve.tensor_tensor(sums_r[64:FAR], src[64:FAR], f32(sums_r)[64:FAR], ALU.subtract).then_inc(sums_lo_done, 1)

            def recip(n, c):
                dve.wait_ge(den_done, DC * n + c + 1)
                if c == 0:
                    dve.wait_ge(ek_turned, n + 1)
                dve.reciprocal(tile(y, c, T), bank(1, c)).then_inc(recip_done, 1)

            def make_y(n):
                for c in range(DC):
                    dve.wait_ge(num_done, DC * n + c + 1)
                    dve.wait_ge(recip_done, DC * n + c + 1)
                    dve.tensor_tensor(tile(y, c, T), bank(2, c), tile(y, c, T), ALU.mult).then_inc(ratio_done, 1)
                dve.wait_ge(gate_q_done, n + 1)
                for c in range(DC):
                    dve.wait_ge(ratio_done, DC * n + c + 1)
                    dve.scalar_tensor_tensor(out=tile(y, c, T), in0=tile(y, c, T), scalar=vec[:, C_BV + c:C_BV + c + 1],
                                             in1=tile(gate_q, c, T), op0=ALU.add, op1=ALU.mult).then_inc(y_done, 1)

            def scale_ff(n):
                dve.wait_ge(rs_done["ff"], n + 1)
                if x1_of(n) is x1:
                    after(dve, out_done, n)
                else:
                    dve.wait_ge(res_done, n)
                for a in range(TT):
                    dve.scalar_tensor_tensor(out=tile(x1_of(n), a), in0=tile(pair(3), a), scalar=mv["ff"][:, 2 * a:2 * a + 1],
                                             in1=gamma_t, op0=ALU.subtract, op1=ALU.mult).then_inc(scaled_done, 1)

            def finish_x1(n):
                dve.wait_ge(x_beta_done, n + 1)
                for a in range(TT):
                    dve.wait_ge(scaled_done, TT * n + a + 1)
                    dve.scalar_tensor_tensor(out=tile(x1_of(n), a), in0=tile(x1_of(n), a), scalar=rs["ff"][:, a:a + 1],
                                             in1=tile(x_beta, a), op0=ALU.mult, op1=ALU.add).then_inc(x1_done, 1)

            def ff_sum(n):
                dve.wait_ge(ff_half_done, n + 1)
                after(dve, norm_done["mid"], most(TT * (n + 2), TT * BATCH))
                for c in range(DC):
                    if c == DC - 1:
                        dve.wait_ge(w2_done, NQ * (n + 1))
                    dve.scalar_tensor_tensor(out=tile(res, c, T), in0=bank(3, c), scalar=vec[:, C_B2 + c:C_B2 + c + 1],
                                             in1=tile(a_t, c, T), op0=ALU.add, op1=ALU.add).then_inc(ff_sum_done, 1)

            def ff_stats(n):
                dve.wait_ge(ff_turned, n + 1)
                row_stats("ff", n, pair(3))

            def fin_stats(n):
                dve.wait_ge(x1_done, TT * (n + 1))
                row_stats("fin", n, x1_of(n))

            def normalise_fin(n):
                dve.wait_ge(mid_turned, most(n + 2, BATCH))
                dve.wait_ge(emb_done, most(n + 4, BATCH))
                dve.wait_ge(nmr_done["fin"], n + 1)
                for a in range(FIN_DVE):
                    dve.tensor_scalar(tile(norm, a), tile(x1_of(n), a), rs["fin"][:, a:a + 1], nmr["fin"][:, a:a + 1],
                                      ALU.mult, ALU.add).then_inc(norm_done["fin"], 1)

            def mixed(n, dst, mu, done, chunks):
                dve.wait_ge(delta_done, n + 1)
                for c in chunks:
                    dve.scalar_tensor_tensor(out=tile(dst, c, T), in0=tile(delta, c, T), scalar=vec[:, mu + c:mu + c + 1],
                                             in1=xn_t[:, c * (T + 1):c * (T + 1) + T], op0=ALU.mult, op1=ALU.add
                                             ).then_inc(done, 1)

            def mix_k(n, chunks=range(DC)):
                dve.wait_ge(norm_done["head"], most(TT * (n + 4), TT * BATCH))
                mixed(n, xk, C_MUK, xk_done, chunks)

            def mix_r(n):
                mixed(n, xr, C_MUR, xr_done, range(DC))

            def square(n):
                dve.wait_ge(relu_k_done, n + 1)
                dve.tensor_tensor(xk, xk, pair(0), ALU.mult).then_inc(sq_done, 1)

            def finish(n):
                dve.wait_ge(fv_done, n + 1)
                dve.wait_ge(tanh_r_done, n + 1)
                dve.scalar_tensor_tensor(out=out_sb, in0=xr, scalar=1.0, in1=pair(0), op0=ALU.add, op1=ALU.mult
                                         ).then_inc(gated_done, 1)
                dve.wait_ge(gated_done, n + 1)
                dve.scalar_tensor_tensor(out=out_sb, in0=out_sb, scalar=gates[:, 1:2], in1=x1_of(n), op0=ALU.mult, op1=ALU.add
                                         ).then_inc(out_done, 1)

            def attention_sum(n, p):
                dve.wait_ge(wo_done, n + 1)
                dve.wait_ge(emb_bo_done, n + 1)
                after(dve, ff_turned, n - 1)
                dve.wait_ge(ev_lo_done, n + 1)
                dve.tensor_tensor(res, pair(2), emb[p], ALU.add).then_inc(res_done, 1)
                dve.wait_ge(res_done, n + 1)
                row_stats("mid", n, res)

            def make_a(n):
                dve.wait_ge(mid_turned, n + 1)
                after(dve, ff_sum_done, DC * n)
                for c in range(DC):
                    dve.tensor_scalar(tile(a_t, c, T), bank(2, c), vec[:, C_GAMMA + c:C_GAMMA + c + 1],
                                      vec[:, C_BETA + c:C_BETA + c + 1], ALU.mult, ALU.add).then_inc(a_done, 1)

            def a_low(n):
                dve.wait_ge(a_hi_done, DC * (n + 1))
                dve.tensor_tensor(a_lo, a_t, f32(a_hi), ALU.subtract).then_inc(a_lo_done, 1)

            def relu_half(n, q):
                j = NQ * n + q
                dve.wait_ge(w1_done, j + 1)
                after(dve, hid_lo_done, j - 1)
                dve.tensor_scalar(hid[q % 2][:, 0:512], bank(HP[q], 0), vec[:, C_B1 + 2 * q:C_B1 + 2 * q + 1], 0.0,
                                  ALU.add, ALU.max).then_inc(relu_dve_done, 1)

            dve.memset(xn_t[:, 0:1], 0.0).then_inc(const_set, 1)
            dve.memset(xn_t[:, T + 1:T + 2], 0.0).then_inc(const_set, 1)
            head_stats(0)
            dve.wait_ge(nmr_done["head"], 1)
            for a in range(TT - FIRST_DVE, TT):
                dve.tensor_scalar(tile(norm, a), tile(x_in, a), rs["head"][:, a:a + 1], nmr["head"][:, a:a + 1],
                                  ALU.mult, ALU.add).then_inc(norm_done["head"], 1)
            make_emb(dve, 0, 0)
            unit_low(0)
            emb_low(0)
            unit_low(1)
            for u in range(2):
                dve.wait_ge(pos_masked, 2 * u + 2)
                dve.tensor_reduce(pos_nmax[:, 2 * u:2 * u + 2], stage[2 + u].rearrange("p (a j) -> p a j", a=2), AX_X,
                                  ALU.max, negate=True).then_inc(pos_max_done, 1)
                if u == 0:
                    head_stats(1)
                    key_max(0)
            unit_low(2)
            dve.wait_ge(far_landed, 16)
            dve.wait_ge(c_col_done, 2)
            for a in range(TT):
                v = tile(far_in, TT + a, FAR)
                dve.tensor_scalar(v, v, c_col[:, a:a + 1], None, ALU.mult).then_inc(far_masked, 1)
            keep_values(0, 3)
            for j in range(TT):
                dve.wait_ge(ew_hi_done, j + 1)
                dve.tensor_tensor(tile(ew_lo, j, WIN), ew_window(j), f32(tile(ew_hi, j, WIN)), ALU.subtract).then_inc(ew_lo_done, 1)
            dve.wait_ge(far_hi_done, 1)
            dve.tensor_tensor(far_c[32:64], bank(1)[32:64], f32(far_c)[32:64], ALU.subtract).then_inc(far_lo_done, 1)
            key_parts(0)
            dve.wait_ge(act_const, 3)
            dve.wait_ge(rows_landed, 48)
            dve.tensor_scalar(gamma_t, gamma_t, gates[:, 0:1], None, ALU.mult).then_inc(dve_const, 1)
            dve.tensor_scalar(beta_t, beta_t, gates[:, 0:1], None, ALU.mult).then_inc(dve_const, 1)
            dve.tensor_scalar(gates[:, 1:2], gates[:, 2:3], 0.5, None, ALU.mult).then_inc(dve_const, 1)
            dve.wait_ge(dve_const, 3)

            def step(i, p):
                a, b, d, e = i - 2, i - 1, i + 1, i + 2
                first = isinstance(i, int) and i == 0
                sums_low(i, 0)
                recip(i, 0)
                if has(a):
                    mix_k(a, [0])
                sums_low(i, 1)
                if has(a):
                    mix_k(a, [1])
                if has(d):
                    emb_low(d)
                recip(i, 1)
                if has(a):
                    mix_r(a)
                make_y(i)
                if first:
                    unit_low(3)
                    unit_low(4)
                if has(a):
                    square(a)
                if has(d):
                    key_max(d)
                if first:
                    unit_low(5)
                if has(b):
                    relu_half(b, 2)
                attention_sum(i, p)
                if has(b):
                    relu_half(b, 3)
                if has(a):
                    finish(a)
                if has(e):
                    head_stats(e)
                if has(b):
                    ff_sum(b)
                make_a(i)
                if has(b):
                    ff_stats(b)
                a_low(i)
                if first:
                    unit_low(6)
                if has(b):
                    scale_ff(b)
                relu_half(i, 0)
                if first:
                    unit_low(7)
                if has(b):
                    finish_x1(b)
                    fin_stats(b)
                relu_half(i, 1)
                if has(d):
                    keep_values(d)
                if has(b):
                    normalise_fin(b)
                if has(d):
                    key_parts(d)

            run_steps(dve, step)
            a, b = BATCH - 2, BATCH - 1
            delta_of(dve, a)
            mix_k(a)
            relu_half(b, 2)
            xk_low(dve, a)
            mix_r(a)
            relu_half(b, 3)
            dve.wait_ge(w2_done, NQ * b + 3)
            hidden_low(dve, b, 3)
            ff_sum(b)
            ff_stats(b)
            square(a)
            scale_ff(b)
            finish_x1(b)
            fin_stats(b)
            normalise_fin(b)
            finish(a)
            delta_of(dve, b)
            mix_k(b)
            mix_r(b)
            xk_low(dve, b)
            xr_low(dve, b)
            square(b)
            sq_low(dve, b)
            finish(b)

        @block.scalar
        def _(act):
            def normalise_tile(kind, src, a):
                act.activation(tile(norm, a), tile(src, a), ACT.Identity, bias=nmr[kind][:, a:a + 1],
                               scale=rs[kind][:, a:a + 1]).then_inc(norm_done[kind], 1)

            def normalise(kind, n, src):
                if kind == "head":
                    after(act, mid_turned, n - 1)
                    after(act, emb_done, n)
                elif kind == "mid":
                    after(act, fin_turned, n - 1)
                    after(act, emb_done, most(n + 2, BATCH))
                else:
                    act.wait_ge(mid_turned, most(n + 2, BATCH))
                    act.wait_ge(emb_done, most(n + 4, BATCH))
                act.wait_ge(nmr_done[kind], n + 1)
                for a in range(FIN_DVE if kind == "fin" else 0, TT):
                    normalise_tile(kind, src, a)

            def unit_high(u):
                act.wait_ge(unit_landed[u], unit_count(u))
                n = unit_cols[u]
                act.activation(w_hi[u][:, :n], stage[UNIT_STAGE[u]][:, :n], ACT.Copy).then_inc(w_hi_done, 1)

            def emb_high(n):
                act.wait_ge(emb_turned, n + 1)
                act.activation(emb_hi, pair(0), ACT.Copy).then_inc(emb_hi_done, 1)

            def exp_keys(n):
                act.wait_ge(kbias_done, n + 1)
                after(act, y_lo_done, n)
                for c in range(DC):
                    act.activation(tile(ek_t, c, T), bank(1, c), ACT.Exp, bias=kbias[:, c:c + 1]).then_inc(ek_done, 1)

            def tanh_q(n, src=1):
                act.wait_ge(q_done, n + 1)
                after(act, y_done, DC * n)
                for c in range(DC):
                    act.activation(tile(gate_q, c, T), bank(src, c), ACT.Tanh, bias=half_bq[:, c:c + 1], scale=0.5
                                   ).then_inc(tanh_q_done, 1)

            def sigmoid_q(n):
                act.wait_ge(tanh_q_done, DC * (n + 1))
                act.activation(gate_q, gate_q, ACT.Copy, bias=0.5, scale=0.5).then_inc(gate_q_done, 1)

            def ek_high(n):
                act.wait_ge(ek_turned, n + 1)
                after(act, wo_done, n)
                act.activation(ek_hi, pair(0), ACT.Copy).then_inc(ek_hi_done, 1)

            def key_sums_high(n):
                act.wait_ge(sums_done, 2 * n + 1)
                after(act, num_done, DC * n)
                act.activation(sums_r[0:FAR], bank(2, 0, D)[0:FAR], ACT.Copy).then_inc(sums_hi_done, 1)

            def keep_sums(n):
                act.wait_ge(sums_done, 2 * n + 2)
                after(act, sums_lo_done, 2 * n)
                act.activation(sums[0:FAR], bank(2, 1, D)[0:FAR], ACT.Copy).then_inc(sums_kept, 1)
                act.wait_ge(den_done, DC * (n + 1))
                act.wait_ge(sums_kept, n + 1)
                act.activation(sums_r[0:FAR], sums[0:FAR], ACT.Copy).then_inc(sums_hi_done, 1)

            def ev_high(n):
                act.wait_ge(ev_done, n + 1)
                after(act, fv_done, n - 2)
                act.activation(ev_hi, val, ACT.Copy).then_inc(ev_hi_done, 1)

            def turned_copy(n):
                act.wait_ge(fin_turned, n + 1)
                after(act, xr_done, DC * n)
                act.activation(xn_t.rearrange("p (c t) -> p c t", c=DC)[:, :, 1:T + 1],
                               pair(2).rearrange("p (c t) -> p c t", c=DC), ACT.Copy).then_inc(xn_t_done, 1)

            def mixed_high(n):
                act.wait_ge(xk_done, DC * (n + 1))
                act.activation(xk_hi, xk, ACT.Copy).then_inc(xk_hi_done, 1)

            def mixed_r_high(n):
                act.wait_ge(xr_done, DC * (n + 1))
                act.activation(xr_hi, xr, ACT.Copy).then_inc(xr_hi_done, 1)

            def relu_k(n):
                act.wait_ge(fk_done, n + 1)
                act.wait_ge(xk_lo_done, n + 1)
                act.activation(xk, pair(0), ACT.Relu).then_inc(relu_k_done, 1)

            def tanh_r(n):
                act.wait_ge(fr_done, n + 1)
                act.activation(xr, pair(2), ACT.Tanh, scale=0.5).then_inc(tanh_r_done, 1)

            def square_high(n):
                act.wait_ge(sq_done, n + 1)
                act.wait_ge(num_done, most(DC * (n + 3), DC * BATCH))
                act.activation(sq_hi, xk, ACT.Copy).then_inc(sq_hi_done, 1)

            def y_high(n):
                act.wait_ge(y_done, DC * (n + 1))
                act.activation(y_hi, y, ACT.Copy).then_inc(y_hi_done, 1)

            def a_high(n):
                after(act, w1_done, NQ * n)
                for c in range(DC):
                    act.wait_ge(a_done, DC * n + c + 1)
                    act.activation(tile(a_hi, c, T), tile(a_t, c, T), ACT.Copy).then_inc(a_hi_done, 1)

            def relu_half(n, q):
                j = NQ * n + q
                act.wait_ge(w1_done, j + 1)
                after(act, hid_lo_done, j - 1)
                act.activation(hid[q % 2][:, 512:PAIR], bank(HP[q], 1), ACT.Relu,
                               bias=vec[:, C_B1 + 2 * q + 1:C_B1 + 2 * q + 2]).then_inc(relu_act_done, 1)

            def hidden_high(n, q):
                j = NQ * n + q
                after(act, w2_done, j - 1)
                act.wait_ge(relu_dve_done, j + 1)
                act.wait_ge(relu_act_done, j + 1)
                act.activation(hid_hi[q % 2], hid[q % 2], ACT.Copy).then_inc(hid_hi_done, 1)

            act.wait_ge(ident_set, 2)
            act.activation(c_col, ident[:, 0:TT], ACT.Tanh).then_inc(c_col_done, 1)
            act.wait_ge(x_landed, 16)
            for u in range(2):
                act.dma_start(stage[2 + u].rearrange("p (a j) -> p a j", a=2),
                              A_pos.rearrange("(a p) j -> p a j", p=P)[:, 2 * u:2 * u + 2]).then_inc(pos_landed[u], 16)
            load_unit(act, 1)
            act.dma_start(gamma_t, A_rows[:, 0:D]).then_inc(rows_landed, 16)
            act.dma_start(beta_t, A_rows[:, D:2 * D]).then_inc(rows_landed, 16)
            act.dma_start(bo_rows, A_rows[:, 2 * D:3 * D]).then_inc(rows_landed, 16)
            act.wait_ge(nmr_done["head"], 1)
            for a in range(TT - FIRST_DVE):
                normalise_tile("head", x_in, a)
            unit_high(0)
            emb_high(0)
            act.wait_ge(vec_landed, 16)
            act.activation(half_bq, vec[:, C_BQ:C_BQ + DC], ACT.Copy, scale=0.5).then_inc(act_const, 1)
            act.activation(gates[:, 0:1], vec[:, C_GX:C_GX + 1], ACT.Tanh).then_inc(act_const, 1)
            act.activation(gates[:, 2:3], vec[:, C_GF:C_GF + 1], ACT.Tanh).then_inc(act_const, 1)
            unit_high(1)
            act.wait_ge(far_landed, 16)
            act.activation(tile_rows, far_in[:, 0:TT * FAR], ACT.Copy).then_inc(tile_rows_done, 1)
            for u in range(2):
                act.wait_ge(pos_max_done, u + 1)
                for a in range(2):
                    v = tile(stage[2 + u], a, T)
                    act.activation(v, v, ACT.Exp, bias=pos_nmax[:, 2 * u + a:2 * u + a + 1]).then_inc(pos_exp_done, 1)
                if u == 0:
                    unit_high(2)
                    exp_keys(0)
            act.wait_ge(c_col_done, 1)
            act.activation(c_col, pos_nmax, ACT.Exp).then_inc(c_col_done, 1)
            act.wait_ge(act_const, 1)
            tanh_q(0, 2)
            ek_high(0)
            for j in range(TT):
                act.wait_ge(pos_turned, j // 2 + 1)
                act.activation(tile(ew_hi, j, WIN), ew_window(j), ACT.Copy).then_inc(ew_hi_done, 1)
            act.wait_ge(far_turned, 1)
            act.activation(far_c[0:FAR], bank(1)[0:FAR], ACT.Copy).then_inc(far_hi_done, 1)
            normalise("head", 1, x_in)
            ev_high(0)
            key_sums_high(0)
            sigmoid_q(0)
            unit_high(3)

            def step(i, p):
                a, b, d, e = i - 2, i - 1, i + 1, i + 2
                first = isinstance(i, int) and i == 0
                if first:
                    unit_high(4)
                if has(b):
                    hidden_high(b, 1)
                if has(d):
                    after(act, v_done, d)
                    emb_high(d)
                keep_sums(i)
                if has(a):
                    mixed_high(a)
                if first:
                    unit_high(5)
                if has(a):
                    mixed_r_high(a)
                    relu_k(a)
                y_high(i)
                if has(a):
                    square_high(a)
                    tanh_r(a)
                if has(d):
                    exp_keys(d)
                if has(b):
                    relu_half(b, 2)
                    hidden_high(b, 2)
                if has(b):
                    relu_half(b, 3)
                    hidden_high(b, 3)
                if first:
                    tanh_q(d)
                normalise("mid", i, res)
                if first:
                    unit_high(6)
                a_high(i)
                if has(e):
                    normalise("head", e, x_in)
                if has(d) and not first:
                    tanh_q(d)
                if first:
                    unit_high(7)
                relu_half(i, 0)
                hidden_high(i, 0)
                relu_half(i, 1)
                if has(b):
                    normalise("fin", b, x1)
                if has(d):
                    ek_high(d)
                if has(b):
                    turned_copy(b)
                if has(d):
                    ev_high(d)
                    key_sums_high(d)
                    sigmoid_q(d)

            run_steps(act, step)
            a, b = BATCH - 2, BATCH - 1
            hidden_high(b, 1)
            mixed_high(a)
            relu_half(b, 2)
            hidden_high(b, 2)
            relu_half(b, 3)
            hidden_high(b, 3)
            act.wait_ge(w2_done, NQ * b + 3)
            mixed_r_high(a)
            relu_k(a)
            tanh_r(a)
            square_high(a)
            normalise("fin", b, x1_of(b))
            turned_copy(b)
            mixed_high(b)
            mixed_r_high(b)
            relu_k(b)
            square_high(b)
            tanh_r(b)

        @block.tensor
        def _(pe):
            def mm(o, s, m, start, stop):
                return pe.matmul(o, s, m, start=start, stop=stop, skip_group_check=True)

            def turn(dst, src, done):
                for c in range(DC):
                    for a in range(TT):
                        last = pe.transpose(bank(dst, c)[:, a * P:(a + 1) * P],
                                            src[:, D * a + c * P:D * a + (c + 1) * P], ident)
                last.then_inc(done, 1)

            def turn_back(dst, src, done):
                for a in range(TT):
                    for c in range(DC):
                        last = pe.transpose(tile(pair(dst), a)[:, c * P:(c + 1) * P],
                                            src[:, T * c + a * P:T * c + (a + 1) * P], ident)
                last.then_inc(done, 1)

            def unit(u, k):
                return w_hi[u][:, 512 * k:512 * (k + 1)], w_lo[u][:, 512 * k:512 * (k + 1)]

            def channels_out(dst, w, act_hi, act_lo, lo_ready, lo_count, done):
                hi, lo = w
                for c in range(DC):
                    for k in range(DC):
                        for r in (hi, lo):
                            mm(bank(dst, c), r[:, D * k + c * P:D * k + (c + 1) * P], tile(act_hi, k, T),
                               k == 0 and r is hi, False)
                pe.wait_ge(lo_ready, lo_count)
                for c in range(DC):
                    for k in range(DC):
                        last = mm(bank(dst, c), hi[:, D * k + c * P:D * k + (c + 1) * P], tile(act_lo, k, T),
                                  False, k == DC - 1)
                last.then_inc(done, 1)

            def rows_out(dst, w, act_hi, act_lo, lo_ready, lo_count, done):
                hi, lo = w
                for a in range(TT):
                    o = tile(pair(dst), a)
                    for k in range(DC):
                        s = act_hi[:, T * k + a * P:T * k + (a + 1) * P]
                        mm(o, s, tile(hi, k), a % 2 == 0 and k == 0, False)
                        mm(o, s, tile(lo, k), False, False)
                pe.wait_ge(lo_ready, lo_count)
                for a in range(TT):
                    o = tile(pair(dst), a)
                    for k in range(DC):
                        s = act_lo[:, T * k + a * P:T * k + (a + 1) * P]
                        last = mm(o, s, tile(hi, k), False, a % 2 == 1 and k == DC - 1)
                last.then_inc(done, 1)

            def relus_read(count):
                after(pe, relu_dve_done, count)
                after(pe, relu_act_done, count)

            def turn_emb(n, p):
                pe.wait_ge(emb_done, n + 1)
                after(pe, ev_done, n)
                turn(0, emb[p], emb_turned)

            def keys(n):
                pe.wait_ge(emb_hi_done, n + 1)
                after(pe, recip_done, DC * n)
                channels_out(1, unit(0, 0), emb_hi, emb_lo, emb_lo_done, n + 1, k_done)

            def queries(n, dst=1):
                if dst == 1:
                    pe.wait_ge(ek_done, DC * (n + 1))
                    relus_read(NQ * (n - 1))
                channels_out(dst, unit(0, 1), emb_hi, emb_lo, emb_lo_done, n + 1, q_done)

            def values(n, dst=1):
                if dst == 1:
                    pe.wait_ge(tanh_q_done, DC * (n + 1))
                rows_out(dst, unit(1, 0), emb_hi, emb_lo, emb_lo_done, n + 1, v_done)

            def turn_keys(n):
                pe.wait_ge(emb_lo_done, n + 1)
                relus_read(NQ * (n - 1) + 1)
                turn_back(0, ek_t, ek_turned)

            def near(dst, c, part, ew, first=False):
                for j in range(TT):
                    o = bank(dst, c)[:, window(j):window(j) + WIN]
                    for w in ew:
                        mm(o, part[:, D * j + c * P:D * j + (c + 1) * P], tile(w, j, WIN),
                           first and j == 0 and w is ew[0], False)

            def weigh(n, part, dst, hi, lo, lo_ready, done):
                near(dst, 0, hi, (ew_hi, ew_lo), True)
                if part == 0:
                    pe.wait_ge(lo_ready, n + 1)
                    near(dst, 0, lo, (ew_hi,))
                    after(pe, xn_t_done, n - 1)
                    relus_read(NQ * (n - 1) + 2)
                o = bank(2, part, D)[0:FAR]
                for p in (hi, lo):
                    if p is lo:
                        pe.wait_ge(lo_ready, n + 1)
                    for j in range(TT):
                        last = mm(o, tile(tile_rows, j, FAR), tile(p, j), p is hi and j == 0, p is lo and j == TT - 1)
                last.then_inc(sums_done, 1)
                if part == 1:
                    near(dst, 0, lo, (ew_hi,))
                    pe.wait_ge(sums_kept, n + 1)
                near(dst, 1, hi, (ew_hi, ew_lo), True)
                near(dst, 1, lo, (ew_hi,))
                pe.wait_ge(sums_hi_done, 2 * n + part + 1)
                pe.wait_ge(sums_lo_done, 2 * n + part + 1)
                for c in range(DC):
                    mm(bank(dst, c), sums_r[0:FAR, c * P:(c + 1) * P], far_c[0:FAR], False, True).then_inc(done, 1)

            def hidden(n, q):
                for b in range(2):
                    m = 2 * q + b
                    for k in range(DC):
                        for w in (w_hi, w_lo):
                            mm(bank(HP[q], b), w[2 + k][:, m * P:(m + 1) * P], tile(a_hi, k, T), k == 0 and w is w_hi, False)
                pe.wait_ge(a_lo_done, n + 1)
                for b in range(2):
                    m = 2 * q + b
                    for k in range(DC):
                        last = mm(bank(HP[q], b), w_hi[2 + k][:, m * P:(m + 1) * P], tile(a_lo, k, T), False, k == DC - 1)
                last.then_inc(w1_done, 1)

            def add_hidden(n, q):
                r = q % 2

                def w2(part, m, c):
                    o = D * (m % 4) + c * P
                    return part[4 + m // 4][:, o:o + P]

                if q == 0:
                    after(pe, scaled_done, TT * n)
                def high(c):
                    for b in range(2):
                        for part in (w_hi, w_lo):
                            mm(bank(3, c), w2(part, 2 * q + b, c), tile(hid_hi[r], b, T),
                               q == 0 and b == 0 and part is w_hi, False)

                def lower(c):
                    for b in range(2):
                        last = mm(bank(3, c), w2(w_hi, 2 * q + b, c), tile(hid_lo[r], b, T),
                                  False, q == NQ - 1 and b == 1)
                    return last

                pe.wait_ge(hid_hi_done, NQ * n + q + 1)
                if q < NQ - 1:
                    high(0)
                    high(1)
                    pe.wait_ge(hid_lo_done, NQ * n + q + 1)
                    lower(0)
                    last = lower(1)
                else:
                    high(0)
                    pe.wait_ge(hid_lo_done, NQ * n + q + 1)
                    lower(0).then_inc(ff_half_done, 1)
                    high(1)
                    last = lower(1)
                last.then_inc(w2_done, 1)

            def turn_fin(n):
                pe.wait_ge(norm_done["fin"], TT * (n + 1))
                relus_read(most(NQ * (n + 1) + 2, NQ * BATCH))
                turn(2, norm, fin_turned)

            def ffn_k(n):
                pe.wait_ge(emb_lo_done, most(n + 4, BATCH))
                pe.wait_ge(xk_hi_done, n + 1)
                channels_out(0, unit(6, 0), xk_hi, xk_lo, xk_lo_done, n + 1, fk_done)

            def ffn_r(n):
                pe.wait_ge(ratio_done, most(DC * (n + 3), DC * BATCH))
                pe.wait_ge(xn_t_done, n + 1)
                pe.wait_ge(xr_hi_done, n + 1)
                rows_out(2, unit(6, 1), xr_hi, xr_lo, xr_lo_done, n + 1, fr_done)

            def ffn_v(n):
                pe.wait_ge(sq_hi_done, n + 1)
                relus_read(most(NQ * (n + 1) + 3, NQ * BATCH))
                rows_out(0, unit(7, 0), sq_hi, sq_lo, sq_lo_done, n + 1, fv_done)

            pe.wait_ge(ident_set, 2)
            turn_emb(0, 0)
            pe.wait_ge(w_lo_done, 1)
            keys(0)
            queries(0, 2)
            pe.wait_ge(w_lo_done, 2)
            values(0, 3)
            pe.wait_ge(ek_done, DC)
            turn_keys(0)
            pe.wait_ge(pos_exp_done, TT)
            for u in range(2):
                pe.wait_ge(*((tanh_q_done, DC) if u == 0 else (val_done, 1)))
                for b in range(2):
                    for a in range(TT):
                        j = 2 * u + b
                        last = pe.transpose(bank(2 + u, b)[:, a * P:(a + 1) * P],
                                            stage[2 + a // 2][:, T * (a % 2) + j * P:T * (a % 2) + (j + 1) * P], ident)
                last.then_inc(pos_turned, 1)
            pe.wait_ge(far_masked, TT)
            for a in range(TT):
                last = pe.transpose(bank(1)[0:FAR, a * P:(a + 1) * P], tile(far_in, TT + a, FAR), ident)
            last.then_inc(far_turned, 1)

            def step(i, p):
                a, b, d = i - 2, i - 1, i + 1
                first = isinstance(i, int) and i == 0
                pe.wait_ge(ek_hi_done, i + 1)
                pe.wait_ge(val_done, i + 1)
                if first:
                    pe.wait_ge(ew_lo_done, TT)
                    pe.wait_ge(tile_rows_done, 1)
                    pe.wait_ge(far_lo_done, 1)
                weigh(i, 0, 1, ek_hi, ek_lo, ek_lo_done, den_done)
                if has(d):
                    turn_emb(d, 1 - p)
                pe.wait_ge(ev_hi_done, i + 1)
                pe.wait_ge(sums_lo_done, 2 * i + 1)
                weigh(i, 1, 2, ev_hi, ev_lo, ev_lo_done, num_done)
                if has(b):
                    add_hidden(b, 1)
                if has(a):
                    if isinstance(a, int) and a == 0:
                        pe.wait_ge(w_lo_done, NU)
                    ffn_k(a)
                if has(d):
                    keys(d)
                if has(a):
                    ffn_r(a)
                if has(b):
                    if has(a):
                        pe.wait_ge(sq_done, a + 1)
                    pe.wait_ge(emb_lo_done, most(b + 3, BATCH))
                    hidden(b, 2)
                if has(a):
                    pe.wait_ge(tanh_r_done, a + 1)
                pe.wait_ge(y_hi_done, i + 1)
                rows_out(2, unit(1, 1), y_hi, y_lo, y_lo_done, i + 1, wo_done)
                if has(b):
                    pe.wait_ge(ek_done, most(DC * (b + 3), DC * BATCH))
                    pe.wait_ge(recip_done, most(DC * (b + 2), DC * BATCH))
                    hidden(b, 3)
                if has(a):
                    ffn_v(a)
                if has(b):
                    add_hidden(b, 2)
                    add_hidden(b, 3)
                if first:
                    queries(d)
                    values(d)
                pe.wait_ge(norm_done["mid"], TT * (i + 1))
                turn(2, norm, mid_turned)
                if has(b):
                    pe.wait_ge(ff_sum_done, DC * (b + 1))
                    turn_back(3, res, ff_turned)
                if has(d) and not first:
                    queries(d)
                pe.wait_ge(a_hi_done, DC * (i + 1))
                if has(a):
                    pe.wait_ge(gated_done, a + 1)
                relus_read(NQ * i - 1)
                if first:
                    pe.wait_ge(w_lo_done, 4)
                    pe.wait_ge(emb_lo_done, 2)
                hidden(i, 0)
                hidden(i, 1)
                if has(d):
                    if not first:
                        values(d)
                    turn_keys(d)
                if first:
                    pe.wait_ge(w_lo_done, 5)
                add_hidden(i, 0)
                if has(b):
                    turn_fin(b)

            run_steps(pe, step)
            a, b = BATCH - 2, BATCH - 1
            hidden(b, 2)
            add_hidden(b, 1)
            pe.wait_ge(recip_done, DC * BATCH)
            hidden(b, 3)
            add_hidden(b, 2)
            add_hidden(b, 3)
            relus_read(NQ * b + 3)
            ffn_k(a)
            pe.wait_ge(ff_sum_done, DC * (b + 1))
            turn_back(3, res, ff_turned)
            ffn_r(a)
            pe.wait_ge(sq_done, a + 1)
            ffn_v(a)
            pe.wait_ge(tanh_r_done, a + 1)
            turn_fin(b)
            pe.wait_ge(gated_done, a + 1)
            ffn_k(b)
            ffn_r(b)
            pe.wait_ge(sq_done, b + 1)
            ffn_v(b)


_SHAPE = (BATCH, T, D)


def kernel(x, ctx_1024, g_xattn, g_ffn, L0_xattn_wq, L0_xattn_bq, L0_xattn_wk, L0_xattn_bk, L0_xattn_wv, L0_xattn_bv,
           L0_xattn_wo, L0_xattn_bo, L0_xattn_pos_bias, L0_xattn_gamma, L0_xattn_beta, L0_xattn_w1, L0_xattn_b1,
           L0_xattn_w2, L0_xattn_b2, L0_ffn_W_r, L0_ffn_W_k, L0_ffn_W_v, L0_ffn_mu_r, L0_ffn_mu_k):
    import numpy as np
    import concourse.bacc as bacc
    from concourse.bass_utils import run_bass_kernel_spmd

    def columns(v):
        return np.asarray(v).reshape(-1, P).T

    vec = np.concatenate([columns(v) for v in (L0_xattn_bq, L0_xattn_bk, L0_xattn_bv, L0_xattn_gamma, L0_xattn_beta,
                                               L0_ffn_mu_r, L0_ffn_mu_k, L0_xattn_b2, L0_xattn_b1)]
                         + [np.broadcast_to(np.asarray(g).reshape(1, 1), (P, 1)) for g in (g_xattn, g_ffn)], axis=1)
    rows = np.broadcast_to(np.concatenate([np.asarray(v) for v in (L0_xattn_gamma, L0_xattn_beta, L0_xattn_bo)])[None, :],
                           (P, 3 * D))
    far = np.zeros((P, 2, TT, FAR), np.float32)
    for j in range(TT):
        outside = (np.arange(T) < window(j)) | (np.arange(T) >= window(j) + WIN)
        for k in range(3):
            far[:, 0, j, 32 * k + j] = 1
            far[:, 1, :, 32 * k + j] = outside.reshape(TT, P).T
    named = {
        "x": x, "ctx": ctx_1024, "vec": vec, "rows": rows, "far": far.reshape(P, -1), "pos": L0_xattn_pos_bias,
        "wk": L0_xattn_wk, "wq": L0_xattn_wq, "wv": L0_xattn_wv, "wo": L0_xattn_wo, "w1": L0_xattn_w1, "w2": L0_xattn_w2,
        "fk": np.asarray(L0_ffn_W_k).T, "fr": np.asarray(L0_ffn_W_r).T, "fv": np.asarray(L0_ffn_W_v).T,
    }
    nc = bacc.Bacc("TRN2", target_bir_lowering=False, num_devices=1)
    arrays, args = {}, []
    for name, a in named.items():
        a = np.ascontiguousarray(a)
        arrays[f"in_{name}"] = a
        args.append(nc.dram_tensor(f"in_{name}", a.shape, mybir.dt.from_np(a.dtype), kind="ExternalInput").ap())
    args.append(nc.dram_tensor("out_0", _SHAPE, F32, kind="ExternalOutput").ap())
    flamingo_gated_block(nc, *args)
    r = run_bass_kernel_spmd(nc, [arrays], core_ids=[0])
    return r.results[0]["out_0"]
```

```python
from contextlib import ExitStack

import concourse.bass as bass
from concourse import mybir

F32 = mybir.dt.float32
F32R = mybir.dt.float32r
ALU = mybir.AluOpType
ACT = mybir.ActivationFunctionType
AX_X = mybir.AxisListType.X

P = 128
BATCH = 8
T = 512
D = 256
H = 1024
BAND = 64
EPS = 1e-5
TT = T // P
DC = D // P
HC = H // P
NQ = HC // 2
PAIR = 1024
HD = 6
WIN = 2 * P
FAR = 64 + TT
FIN_DVE = 3
FIRST_DVE = 2
NU = 8

C_BQ, C_BK, C_BV, C_GAMMA, C_BETA, C_MUR, C_MUK, C_B1 = range(0, 8 * DC, DC)
C_GX = C_B1 + HC
C_GF = C_GX + 1
NVEC = C_GF + 1


def window(j):
    return min(max(j * P - BAND, 0), T - WIN)


def flamingo_gated_block(nc, A_x, A_ctx, A_vec, A_rows, A_far, A_pos, A_wk, A_wq, A_wv, A_wo,
                         A_w1, A_w2, A_fk, A_fr, A_fv, out):
    ctx = ExitStack()
    with ctx:
        def sb(name, cols, dt=F32):
            return ctx.enter_context(nc.sbuf_tensor(name, [P, cols], dt))[:, :]

        def sem(name):
            return ctx.enter_context(nc.semaphore(name))

        ident = sb("ident", P)
        vec = sb("vec", NVEC)
        half_bq = sb("half_bq", DC)
        gates = sb("gates", 3)
        gamma_t = sb("gamma_t", D)
        beta_t = sb("beta_t", D)
        bo_rows = sb("bo_rows", D)
        gamma_rows = sb("gamma_rows", D)
        bias_rows = sb("bias_rows", D)
        minus_half, minus_one, eps_col = sb("minus_half", TT), sb("minus_one", TT), sb("eps_col", TT)
        unit_cols = [PAIR] * (NU - 1) + [DC * D]
        w_hi = [sb(f"w_hi{u}", unit_cols[u], F32R) for u in range(NU)]
        w_lo = [sb(f"w_lo{u}", unit_cols[u], F32R) for u in range(NU)]
        ew_hi = sb("ew_hi", TT * WIN, F32R)
        ew_lo = sb("ew_lo", TT * WIN, F32R)
        far_in = sb("far_in", 2 * TT * FAR)
        tile_rows = sb("tile_rows", TT * FAR, F32R)
        far_c = sb("far_c", T, F32R)
        c_col = sb("c_col", TT)
        sums, sums_r = sb("sums", D), sb("sums_r", D, F32R)
        ek_sums = sb("ek_sums", DC * TT)
        ek_rows = sb("ek_rows", DC * 96)
        pos_nmax = sb("pos_nmax", TT)

        emb = [sb(f"emb{p}", TT * D) for p in range(2)]
        norm = sb("norm", TT * D)
        emb_hi, emb_lo = sb("emb_hi", DC * T, F32R), sb("emb_lo", DC * T, F32R)
        y = sb("y", DC * T)
        ek_t = y
        gate_q = sb("gate_q", DC * T)
        ek_hi, ek_lo = sb("ek_hi", TT * D, F32R), sb("ek_lo", TT * D, F32R)
        y_hi, y_lo = ek_hi, ek_lo
        ev_hi, ev_lo = sb("ev_hi", TT * D, F32R), sb("ev_lo", TT * D, F32R)
        sq_hi, sq_lo = ev_hi, ev_lo
        res = sb("res", TT * D)
        val = res
        a_t = sb("a_t", DC * T)
        a_rows = [sb(f"a_rows{p}", TT * D) for p in range(2)]
        a_hi, a_lo = sb("a_hi", DC * T, F32R), sb("a_lo", DC * T, F32R)
        hid = [sb(f"hid{r}", PAIR) for r in range(2)]
        hid_hi = [sb(f"hid_hi{r}", PAIR, F32R) for r in range(2)]
        hid_lo = [sb(f"hid_lo{r}", PAIR, F32R) for r in range(2)]
        x_beta = sb("x_beta", TT * D)
        x1 = sb("x1", TT * D)
        xn_t = sb("xn_t", DC * (T + 1))
        x_in = sb("x_in", TT * D)
        xk = x_in
        xk_hi, xk_lo = sb("xk_hi", DC * T, F32R), sb("xk_lo", DC * T, F32R)
        xr = sb("xr", DC * T)
        xr_hi, xr_lo = hid_hi[0], hid_lo[0]
        out_sb = sb("out_sb", TT * D)
        stage = [hid[0], hid[1], x1, out_sb]
        UNIT_STAGE = [0, 1, 0, 1, 2, 3, 2, 3]

        KINDS = ("head", "mid", "ff", "fin")
        st = {k: sb(f"st_{k}", TT * HD) for k in KINDS}
        mv = {k: sb(f"mv_{k}", TT * 2) for k in KINDS}
        ve = {k: sb(f"ve_{k}", TT) for k in KINDS}
        nm = {k: sb(f"nm_{k}", TT) for k in KINDS}
        rs = {k: sb(f"rs_{k}", TT) for k in KINDS}
        nmr = {k: sb(f"nmr_{k}", TT) for k in KINDS}
        held = sb("held", 1)
        kmax, kshift, kbias = sb("kmax", DC), sb("kshift", DC), sb("kbias", DC)

        ps = ctx.enter_context(nc.psum_tensor("ps", [P, 4 * PAIR], F32))

        def bank(pair, b=0, n=512):
            o = pair * PAIR + 512 * b
            return ps[:, o:o + n]

        def pair(k):
            return ps[:, k * PAIR:(k + 1) * PAIR]

        x_landed, ctx_landed, again_landed, out_stored = (sem("x_landed"), sem("ctx_landed"), sem("again_landed"),
                                                             sem("out_stored"))
        vec_landed, rows_landed, far_landed = sem("vec_landed"), sem("rows_landed"), sem("far_landed")
        tile_rows_done, c_col_done, far_masked, far_turned = (sem("tile_rows_done"), sem("c_col_done"),
                                                              sem("far_masked"), sem("far_turned"))
        far_hi_done, far_lo_done = sem("far_hi_done"), sem("far_lo_done")
        ek_summed, ek_rows_done = sem("ek_summed"), sem("ek_rows_done")
        sums_done, sums_kept, sums_hi_done, sums_lo_done = (sem("sums_done"), sem("sums_kept"), sem("sums_hi_done"),
                                                            sem("sums_lo_done"))
        unit_landed = [sem(f"unit_landed{u}") for u in range(NU)]
        pos_landed = [sem(f"pos_landed{u}") for u in range(2)]
        ident_set, const_set, dve_const, act_const = sem("ident_set"), sem("const_set"), sem("dve_const"), sem("act_const")
        w_hi_done, w_lo_done = sem("w_hi_done"), sem("w_lo_done")
        pos_masked, pos_max_done, pos_exp_done = sem("pos_masked"), sem("pos_max_done"), sem("pos_exp_done")
        pos_turned, ew_hi_done, ew_lo_done = sem("pos_turned"), sem("ew_hi_done"), sem("ew_lo_done")
        st_done = {k: sem(f"st_{k}_done") for k in KINDS}
        mv_done = {k: sem(f"mv_{k}_done") for k in KINDS}
        ve_done = {k: sem(f"ve_{k}_done") for k in KINDS}
        rs_done = {k: sem(f"rs_{k}_done") for k in KINDS}
        nmr_done = {k: sem(f"nmr_{k}_done") for k in KINDS}
        norm_done = {k: sem(f"norm_{k}_done") for k in ("head", "mid", "fin")}
        emb_bo_done, ff_sum_done = sem("emb_bo_done"), sem("ff_sum_done")
        a_scaled_done, a_rows_done = sem("a_scaled_done"), sem("a_rows_done")
        emb_done, emb_turned, emb_hi_done, emb_lo_done = (sem("emb_done"), sem("emb_turned"), sem("emb_hi_done"),
                                                          sem("emb_lo_done"))
        k_done, kmax_done, kshift_done, kbias_done = sem("k_done"), sem("kmax_done"), sem("kshift_done"), sem("kbias_done")
        ek_done, v_done, q_done, val_done, tanh_q_done, gate_q_done = (sem("ek_done"), sem("v_done"), sem("q_done"),
                                                                     sem("val_done"), sem("tanh_q_done"), sem("gate_q_done"))
        ek_turned, ek_hi_done, ek_lo_done = sem("ek_turned"), sem("ek_hi_done"), sem("ek_lo_done")
        ev_done, ev_hi_done, ev_lo_done = sem("ev_done"), sem("ev_hi_done"), sem("ev_lo_done")
        den_done, num_done, recip_done, ratio_done = sem("den_done"), sem("num_done"), sem("recip_done"), sem("ratio_done")
        y_done, y_hi_done, y_lo_done = sem("y_done"), sem("y_hi_done"), sem("y_lo_done")
        wo_half_done, fv_half_done = sem("wo_half_done"), sem("fv_half_done")
        res_half_done, emb_half_done = sem("res_half_done"), sem("emb_half_done")
        wo_done, res_done, mid_turned = sem("wo_done"), sem("res_done"), sem("mid_turned")
        a_done, a_hi_done, a_lo_done = sem("a_done"), sem("a_hi_done"), sem("a_lo_done")
        w1_done, relu_dve_done, relu_act_done = sem("w1_done"), sem("relu_dve_done"), sem("relu_act_done")
        hid_hi_done, hid_lo_done, w2_done, ff_half_done = (sem("hid_hi_done"), sem("hid_lo_done"), sem("w2_done"),
                                                           sem("ff_half_done"))
        x_beta_done, scaled_done, x1_done = sem("x_beta_done"), sem("scaled_done"), sem("x1_done")
        fin_turned, xn_t_done, delta_done = sem("fin_turned"), sem("xn_t_done"), sem("delta_done")
        xk_done, xr_done = sem("xk_done"), sem("xr_done")
        xk_hi_done, xk_lo_done, xr_hi_done, xr_lo_done = (sem("xk_hi_done"), sem("xk_lo_done"), sem("xr_hi_done"),
                                                              sem("xr_lo_done"))
        fk_done, fr_done, fv_done = sem("fk_done"), sem("fr_done"), sem("fv_done")
        relu_k_done, sq_done, sq_hi_done, sq_lo_done, tanh_r_done = (sem("relu_k_done"), sem("sq_done"), sem("sq_hi_done"),
                                                                   sem("sq_lo_done"), sem("tanh_r_done"))
        gated_done, out_done = sem("gated_done"), sem("out_done")

        def after(eng, s, count):
            if not isinstance(count, int) or count > 0:
                eng.wait_ge(s, count)

        def most(count, top):
            return min(count, top) if isinstance(count, int) else count

        def has(n):
            return not isinstance(n, int) or 0 <= n < BATCH

        def f32(ap):
            return ap.bitcast(F32)

        def tile(ap, a, n=D):
            return ap[:, a * n:(a + 1) * n]

        def low(eng, dst, src, hi, ready, count, done):
            eng.wait_ge(ready, count)
            eng.tensor_tensor(dst, src, f32(hi), ALU.subtract).then_inc(done, 1)

        def hidden_low(eng, n, q):
            low(eng, hid_lo[q % 2], hid[q % 2], hid_hi[q % 2], hid_hi_done, NQ * n + q + 1, hid_lo_done)

        def xk_low(eng, n):
            low(eng, xk_lo, xk, xk_hi, xk_hi_done, DC * (n + 1), xk_lo_done)

        def xr_low(eng, n):
            low(eng, xr_lo, xr_of(n), xr_hi, xr_hi_done, n + 1, xr_lo_done)

        def y_low(eng, n):
            low(eng, y_lo, y, y_hi, y_hi_done, n + 1, y_lo_done)

        def sq_low(eng, n):
            low(eng, sq_lo, xk, sq_hi, sq_hi_done, n + 1, sq_lo_done)

        def make_emb(eng, n, p):
            eng.wait_ge(ctx_landed, 16 * (n + 1))
            eng.wait_ge(norm_done["head"], TT * (n + 1))
            eng.tensor_tensor(emb[p], norm, emb[p], ALU.add).then_inc(emb_done, 1)

        def is_last(n):
            return isinstance(n, int) and n == BATCH - 1

        def delta_buf(n):
            return x_beta if is_last(n) else out_sb

        def delta_of(eng, n, chunks=range(DC)):
            if is_last(n):
                eng.wait_ge(x1_done, TT * BATCH)
            else:
                after(eng, out_stored, 16 * n)
            for c in chunks:
                o = c * (T + 1)
                eng.wait_ge(xn_t_done, DC * n + c + 1)
                eng.tensor_tensor(tile(delta_buf(n), c, T), xn_t[:, o + 1:o + 1 + T], xn_t[:, o:o + T],
                                  ALU.subtract).then_inc(delta_done, 1)

        def key_pair(n):
            return 1 if is_last(n) else 0

        def xr_of(n):
            return gate_q if is_last(n) else xr

        def out_of(n):
            return xr_of(n) if is_last(n) else out_sb

        def x1_of(n):
            return emb[BATCH % 2] if is_last(n) else x1

        def run_steps(eng, step):
            step(0, 0)
            step(1, 1)
            with eng.Fori(1, 3) as i:
                step(2 * i, 0)
                step(2 * i + 1, 1)
            for n in range(BATCH - 2, BATCH):
                step(n, n % 2)

        def ew_window(j):
            return bank(2 + j // 2, j % 2)[:, window(j):window(j) + WIN]

        HP = [0, 2, 0, 1]
        block = ctx.enter_context(nc.Block())

        def rows_of(a, n):
            return a.rearrange("b (a p) d -> p b a d", p=P)[:, bass.ds(n, 1)]

        SQUARES = {0: (A_wk, A_wq), 1: (A_wv, A_wo), 6: (A_fk, A_fr), 7: (A_fv,)}

        def load_unit(eng, u):
            dst = stage[UNIT_STAGE[u]]
            if u in SQUARES:
                for k, a in enumerate(SQUARES[u]):
                    eng.dma_start(dst[:, 512 * k:512 * (k + 1)].rearrange("p (c n) -> p c n", c=DC),
                                  a.rearrange("(c p) n -> p c n", p=P)).then_inc(unit_landed[u], 16)
            elif u < 4:
                eng.dma_start(dst, A_w1[(u - 2) * P:(u - 1) * P, :]).then_inc(unit_landed[u], 16)
            else:
                eng.dma_start(dst.rearrange("p (c n) -> p c n", c=4),
                              A_w2.rearrange("(c p) n -> p c n", p=P)[:, 4 * (u - 4):4 * (u - 3)]
                              ).then_inc(unit_landed[u], 16)

        def unit_count(u):
            return 16 * (len(SQUARES[u]) if u in SQUARES else 1)

        @block.sync
        def _(sp):
            def batch_dma(sb_tile, dram, n):
                return sb_tile.rearrange("p (b a d) -> p b a d", b=1, a=TT), rows_of(dram, n)

            def load_x(n):
                if has(n - 4) and not (isinstance(n, int) and n < 4):
                    sp.wait_ge(sq_lo_done, n - 3)
                after(sp, norm_done["head"], TT * n)
                sp.dma_start(*batch_dma(x_in, A_x, n)).then_inc(x_landed, 16)

            def load_ctx(n, p):
                after(sp, res_done, n - 1)
                after(sp, emb_done, n)
                sp.dma_start(*batch_dma(emb[p], A_ctx, n)).then_inc(ctx_landed, 16)

            def load_again(n):
                after(sp, x1_done, TT * n)
                sp.dma_start(*batch_dma(x_beta, A_x, n)).then_inc(again_landed, 16)

            def store(n):
                sp.wait_ge(out_done, n + 1)
                sp.dma_start(rows_of(out, n), out_sb.rearrange("p (b a d) -> p b a d", b=1, a=TT)).then_inc(out_stored, 16)

            load_x(0)
            load_ctx(0, 0)
            load_unit(sp, 0)
            sp.dma_start(vec, A_vec).then_inc(vec_landed, 16)
            sp.dma_start(far_in, A_far).then_inc(far_landed, 16)
            for k, row in ((2, bo_rows), (0, gamma_t), (0, gamma_rows), (1, beta_t), (3, bias_rows)):
                sp.dma_start(row, A_rows[:, k * D:(k + 1) * D]).then_inc(rows_landed, 16)
            load_x(1)
            load_ctx(1, 1)
            for u in (2, 3):
                sp.wait_ge(w_lo_done, u - 1)
                load_unit(sp, u)
            sp.wait_ge(pos_turned, 2)
            load_unit(sp, 4)
            load_unit(sp, 5)

            def step(i, p):
                if has(i - 1):
                    load_again(i - 1)
                if has(i + 2):
                    load_x(i + 2)
                    load_ctx(i + 2, p)
                if isinstance(i, int) and i == 0:
                    for u in (6, 7):
                        sp.wait_ge(w_lo_done, u - 1)
                        load_unit(sp, u)
                if has(i - 2):
                    store(i - 2)

            run_steps(sp, step)
            load_again(BATCH - 1)
            store(BATCH - 2)
            for h in range(2):
                sp.wait_ge(out_done, BATCH + h)
                sp.dma_start(rows_of(out, BATCH - 1)[:, :, 2 * h:2 * h + 2],
                             tile(out_of(BATCH - 1), h, PAIR // 2).rearrange("p (b a d) -> p b a d", b=1, a=2)).then_inc(out_stored, 16)
            sp.wait_ge(out_stored, 16 * (BATCH + 1))

        @block.gpsimd
        def _(pool):
            def stats(kind, n):
                mvs = mv[kind].rearrange("p (a s) -> p s a", s=2)
                pool.wait_ge(mv_done[kind], TT * (n + 1))
                after(pool, nmr_done[kind], n)
                pool.tensor_tensor(ve[kind], mvs[:, 1], eps_col, ALU.add).then_inc(ve_done[kind], 1)
                pool.tensor_tensor(nm[kind], mvs[:, 0], minus_one, ALU.mult).then_inc(ve_done[kind], 1)
                pool.wait_ge(ve_done[kind], 2 * (n + 1))
                if kind == "ff":
                    after(pool, x1_done, TT * n)
                else:
                    after(pool, norm_done[kind], TT * n)
                pool.tensor_tensor(rs[kind], ve[kind], minus_half, ALU.pow).then_inc(rs_done[kind], 1)
                pool.wait_ge(rs_done[kind], n + 1)
                pool.tensor_tensor(nmr[kind], nm[kind], rs[kind], ALU.mult).then_inc(nmr_done[kind], 1)

            def with_row(dst, src, row, op, done):
                r = row.rearrange("p (o d) -> p o d", o=1).to_broadcast([P, TT, D])
                pool.tensor_tensor(dst.rearrange("p (a d) -> p a d", a=TT), src.rearrange("p (a d) -> p a d", a=TT), r, op
                                   ).then_inc(done, 1)

            def add_row(ap, row, done):
                with_row(ap, ap, row, ALU.add, done)

            def scale_a(n, p):
                pool.wait_ge(norm_done["mid"], TT * (n + 1))
                after(pool, ff_sum_done, DC * (n - 1))
                with_row(a_rows[p], norm, gamma_rows, ALU.mult, a_scaled_done)

            def finish_a(n, p):
                pool.wait_ge(a_scaled_done, n + 1)
                add_row(a_rows[p], bias_rows, a_rows_done)

            def emb_plus_bo(n, p):
                pool.wait_ge(emb_turned, n + 1)
                pool.wait_ge(rows_landed, 16 * 5)
                add_row(emb[p], bo_rows, emb_bo_done)

            def x_plus_beta(n):
                pool.wait_ge(dve_const, 3)
                pool.wait_ge(again_landed, 16 * (n + 1))
                add_row(x_beta, beta_t, x_beta_done)

            def ev_low(n):
                low(pool, ev_lo, val, ev_hi, ev_hi_done, n + 1, ev_lo_done)

            pool.memset(ident, 0.0).then_inc(ident_set, 1)
            pool.wait_ge(ident_set, 1)
            pool.affine_select(out=ident, in_=ident, compare_op=ALU.not_equal, fill=1.0, base=0,
                               pattern=[[-1, P]], channel_multiplier=1).then_inc(ident_set, 1)
            pool.memset(minus_half, -0.5).then_inc(ident_set, 1)
            pool.memset(minus_one, -1.0).then_inc(ident_set, 1)
            pool.memset(eps_col, EPS).then_inc(ident_set, 1)
            pool.wait_ge(ident_set, 5)
            stats("head", 0)
            for u in range(2):
                v = stage[2 + u].rearrange("p (a j) -> p a j", a=2)
                pool.wait_ge(pos_landed[u], 16)
                pool.affine_select(out=v, in_=v, compare_op=ALU.is_gt, fill=0.0, base=BAND + 2 * u * P,
                                   pattern=[[P, 2], [-1, T]], channel_multiplier=1).then_inc(pos_masked, 1)
                pool.wait_ge(pos_masked, 2 * u + 1)
                pool.affine_select(out=v, in_=v, compare_op=ALU.is_gt, fill=0.0, base=BAND - 2 * u * P,
                                   pattern=[[-P, 2], [1, T]], channel_multiplier=-1).then_inc(pos_masked, 1)
            emb_plus_bo(0, 0)
            stats("head", 1)
            make_emb(pool, 1, 1)

            def step(i, p):
                a, b, d, e = i - 2, i - 1, i + 1, i + 2
                ev_low(i)
                if has(a):
                    delta_of(pool, a)
                if has(b):
                    hidden_low(pool, b, 1)
                if has(a):
                    xk_low(pool, a)
                    xr_low(pool, a)
                if has(d):
                    emb_plus_bo(d, 1 - p)
                if not (isinstance(i, int) and i == 0):
                    y_low(pool, i)
                if has(a):
                    sq_low(pool, a)
                if has(b):
                    x_plus_beta(b)
                    hidden_low(pool, b, 2)
                stats("mid", i)
                if has(b):
                    hidden_low(pool, b, 3)
                scale_a(i, p)
                if has(e):
                    stats("head", e)
                if has(b):
                    stats("ff", b)
                if has(e):
                    make_emb(pool, e, p)
                hidden_low(pool, i, 0)
                if has(b):
                    stats("fin", b)
                finish_a(i, p)

            run_steps(pool, step)
            a, b = BATCH - 2, BATCH - 1
            hidden_low(pool, b, 1)
            hidden_low(pool, b, 2)
            x_plus_beta(b)
            xr_low(pool, a)
            stats("ff", b)
            pool.wait_ge(relu_k_done, a + 1)
            pool.tensor_tensor(xk, xk, xk, ALU.mult).then_inc(sq_done, 1)
            stats("fin", b)

        @block.vector
        def _(dve):
            def row_stats(kind, n, src, between=None):
                after(dve, mv_done[kind], TT * n)
                for a in range(TT):
                    dve.bn_stats(tile(st[kind], a, HD), tile(src, a)).then_inc(st_done[kind], 1)
                if between is not None:
                    between()
                dve.wait_ge(st_done[kind], TT * (n + 1))
                after(dve, ve_done[kind], 2 * n)
                if kind == "ff":
                    after(dve, scaled_done, TT * n)
                dve.memset(held, 0.0)
                for a in range(TT):
                    dve.bn_aggr(tile(mv[kind], a, 2), tile(st[kind], a, HD)).then_inc(mv_done[kind], 1)

            def head_stats(n):
                dve.wait_ge(x_landed, 16 * (n + 1))
                row_stats("head", n, x_in)

            def emb_low(n):
                dve.wait_ge(emb_hi_done, n + 1)
                dve.tensor_tensor(emb_lo, pair(0), f32(emb_hi), ALU.subtract).then_inc(emb_lo_done, 1)

            def key_max(n, src=1):
                dve.wait_ge(k_done, n + 1)
                after(dve, kshift_done, n)
                dve.tensor_reduce(kmax, pair(src).rearrange("p (c t) -> p c t", c=DC), AX_X, ALU.max).then_inc(kmax_done, 1)
                dve.wait_ge(kmax_done, n + 1)
                after(dve, kbias_done, n)
                dve.tensor_tensor(kshift, kmax, vec[:, C_BK:C_BK + DC], ALU.add).then_inc(kshift_done, 1)
                dve.wait_ge(kshift_done, n + 1)
                after(dve, ek_done, DC * n)
                dve.tensor_tensor(kbias, vec[:, C_BK:C_BK + DC], kshift, ALU.subtract).then_inc(kbias_done, 1)

            def pos_max(u):
                dve.wait_ge(pos_masked, 2 * u + 2)
                dve.tensor_reduce(pos_nmax[:, 2 * u:2 * u + 2], stage[2 + u].rearrange("p (a j) -> p a j", a=2), AX_X,
                                  ALU.max, negate=True).then_inc(pos_max_done, 1)

            def keep_values(n, src=1):
                dve.wait_ge(v_done, n + 1)
                after(dve, scaled_done, TT * (n - 1))
                after(dve, norm_done["mid"], TT * n)
                dve.tensor_copy(val, pair(src)).then_inc(val_done, 1)

            def sum_keys(n):
                after(dve, ek_rows_done, n)
                for c in range(DC):
                    dve.wait_ge(ek_done, DC * n + c + 1)
                    dve.tensor_reduce(tile(ek_sums, c, TT), tile(ek_t, c, T).rearrange("p (j t) -> p j t", j=TT), AX_X,
                                      ALU.add).then_inc(ek_summed, 1)
                dve.wait_ge(ek_summed, DC * (n + 1))
                after(dve, sums_done, 2 * n)
                dve.tensor_copy(ek_rows.rearrange("p (c k r) -> p c k r", c=DC, k=3)[:, :, :, 0:TT],
                                ek_sums.rearrange("p (c k j) -> p c k j", c=DC, k=1).to_broadcast([P, DC, 3, TT])
                                ).then_inc(ek_rows_done, 1)

            def keys_low(n):
                dve.wait_ge(ek_hi_done, n + 1)
                dve.tensor_tensor(ek_lo, pair(0), f32(ek_hi), ALU.subtract).then_inc(ek_lo_done, 1)

            def weigh_values(n):
                dve.wait_ge(val_done, n + 1)
                dve.tensor_tensor(val, pair(0), val, ALU.mult).then_inc(ev_done, 1)

            def unit_low(u):
                dve.wait_ge(w_hi_done, u + 1)
                n = unit_cols[u]
                dve.tensor_tensor(w_lo[u][:, :n], stage[UNIT_STAGE[u]][:, :n], f32(w_hi[u])[:, :n],
                                  ALU.subtract).then_inc(w_lo_done, 1)

            def sums_low(n, part):
                dve.wait_ge(sums_hi_done, 2 * n + part + 1)
                src = sums if part == 1 else bank(2, 0, D)
                dve.tensor_tensor(sums_r[64:FAR], src[64:FAR], f32(sums_r)[64:FAR], ALU.subtract).then_inc(sums_lo_done, 1)

            def recip(n, c):
                dve.wait_ge(den_done, DC * n + c + 1)
                if c == 0:
                    dve.wait_ge(ek_turned, n + 1)
                dve.reciprocal(tile(y, c, T), bank(1, c)).then_inc(recip_done, 1)

            def make_y(n):
                for c in range(DC):
                    dve.wait_ge(num_done, DC * n + c + 1)
                    dve.wait_ge(recip_done, DC * n + c + 1)
                    dve.tensor_tensor(tile(y, c, T), bank(2, c), tile(y, c, T), ALU.mult).then_inc(ratio_done, 1)
                dve.wait_ge(gate_q_done, n + 1)
                for c in range(DC):
                    dve.wait_ge(ratio_done, DC * n + c + 1)
                    dve.scalar_tensor_tensor(out=tile(y, c, T), in0=tile(y, c, T), scalar=vec[:, C_BV + c:C_BV + c + 1],
                                             in1=tile(gate_q, c, T), op0=ALU.add, op1=ALU.mult).then_inc(y_done, 1)

            def scale_ff(n):
                dve.wait_ge(mv_done["ff"], TT * (n + 1))
                if x1_of(n) is x1:
                    after(dve, out_done, n)
                else:
                    dve.wait_ge(res_done, n)
                for a in range(TT):
                    dve.scalar_tensor_tensor(out=tile(x1_of(n), a), in0=tile(res, a), scalar=mv["ff"][:, 2 * a:2 * a + 1],
                                             in1=gamma_t, op0=ALU.subtract, op1=ALU.mult).then_inc(scaled_done, 1)

            def finish_x1(n):
                dve.wait_ge(rs_done["ff"], n + 1)
                dve.wait_ge(x_beta_done, n + 1)
                for a in range(TT):
                    dve.wait_ge(scaled_done, TT * n + a + 1)
                    dve.scalar_tensor_tensor(out=tile(x1_of(n), a), in0=tile(x1_of(n), a), scalar=rs["ff"][:, a:a + 1],
                                             in1=tile(x_beta, a), op0=ALU.mult, op1=ALU.add).then_inc(x1_done, 1)

            def ff_sum(n, p):
                after(dve, norm_done["mid"], most(TT * (n + 2), TT * BATCH))
                dve.wait_ge(a_rows_done, n + 1)
                for h in range(2):
                    dve.wait_ge(*((ff_half_done, n + 1) if h == 0 else (w2_done, NQ * (n + 1))))
                    dve.tensor_tensor(tile(res, h, 2 * D), bank(3, h), tile(a_rows[p], h, 2 * D), ALU.add
                                      ).then_inc(ff_sum_done, 1)

            def ff_stats(n, between=None):
                dve.wait_ge(ff_sum_done, DC * (n + 1))
                row_stats("ff", n, res, between)

            def fin_stats(n):
                dve.wait_ge(x1_done, TT * (n + 1))
                row_stats("fin", n, x1_of(n))

            def normalise_tiles(kind, src, tiles):
                for a in tiles:
                    dve.tensor_scalar(tile(norm, a), tile(src, a), rs[kind][:, a:a + 1], nmr[kind][:, a:a + 1],
                                      ALU.mult, ALU.add).then_inc(norm_done[kind], 1)

            def normalise_fin(n):
                dve.wait_ge(mid_turned, most(n + 2, BATCH))
                dve.wait_ge(emb_done, most(n + 4, BATCH))
                dve.wait_ge(a_scaled_done, most(n + 2, BATCH))
                dve.wait_ge(nmr_done["fin"], n + 1)
                normalise_tiles("fin", x1_of(n), range(FIN_DVE))

            def mixed(n, dst, mu, done, chunks):
                for c in chunks:
                    dve.wait_ge(delta_done, DC * n + c + 1)
                    dve.scalar_tensor_tensor(out=tile(dst, c, T), in0=tile(delta_buf(n), c, T), scalar=vec[:, mu + c:mu + c + 1],
                                             in1=xn_t[:, c * (T + 1):c * (T + 1) + T], op0=ALU.mult, op1=ALU.add
                                             ).then_inc(done, 1)

            def mix_k(n, chunks=range(DC)):
                dve.wait_ge(norm_done["head"], most(TT * (n + 4), TT * BATCH))
                mixed(n, xk, C_MUK, xk_done, chunks)

            def mix_r(n, chunks=range(DC)):
                mixed(n, xr_of(n), C_MUR, xr_done, chunks)

            def square(n):
                dve.wait_ge(relu_k_done, n + 1)
                dve.tensor_tensor(xk, xk, pair(key_pair(n)), ALU.mult).then_inc(sq_done, 1)

            def gate_ffn(n, parts=1, h=0):
                def part(ap):
                    return tile(ap, h, PAIR // parts)

                dve.wait_ge(*((fv_half_done, 2) if parts == 2 and h == 0 else (fv_done, n + 1)))
                dve.wait_ge(tanh_r_done, n + 1)
                dve.scalar_tensor_tensor(out=part(out_of(n)), in0=part(xr_of(n)), scalar=1.0, in1=part(pair(0)),
                                         op0=ALU.add, op1=ALU.mult).then_inc(gated_done, 1)

            def make_out(n, parts=1, h=0):
                def part(ap):
                    return tile(ap, h, PAIR // parts)

                dve.wait_ge(gated_done, n + h + 1)
                dve.scalar_tensor_tensor(out=part(out_of(n)), in0=part(out_of(n)), scalar=gates[:, 1:2],
                                         in1=part(x1_of(n)), op0=ALU.mult, op1=ALU.add).then_inc(out_done, 1)

            def attention_sum(n, p):
                dve.wait_ge(wo_done, n + 1)
                dve.wait_ge(emb_bo_done, n + 1)
                after(dve, scaled_done, TT * (n - 1))
                dve.wait_ge(ev_lo_done, n + 1)
                dve.tensor_tensor(res, pair(2), emb[p], ALU.add).then_inc(res_done, 1)
                dve.wait_ge(res_done, n + 1)
                row_stats("mid", n, res)

            def first_attention_sum():
                dve.wait_ge(emb_bo_done, 1)
                dve.wait_ge(ev_lo_done, 1)
                for h in range(2):
                    dve.wait_ge(*((wo_half_done, 1) if h == 0 else (wo_done, 1)))
                    dve.tensor_tensor(tile(res, h, 2 * D), bank(2, h), tile(emb[0], h, 2 * D), ALU.add
                                      ).then_inc(*((res_half_done, 1) if h == 0 else (res_done, 1)))
                    dve.wait_ge(*((res_half_done, 1) if h == 0 else (res_done, 1)))
                    for a in range(2 * h, 2 * h + 2):
                        dve.bn_stats(tile(st["mid"], a, HD), tile(res, a)).then_inc(st_done["mid"], 1)
                dve.wait_ge(st_done["mid"], TT)
                dve.memset(held, 0.0)
                for a in range(TT):
                    dve.bn_aggr(tile(mv["mid"], a, 2), tile(st["mid"], a, HD)).then_inc(mv_done["mid"], 1)

            def make_a(n):
                dve.wait_ge(mid_turned, n + 1)
                after(dve, a_hi_done, DC * n)
                after(dve, a_lo_done, n)
                for c in range(DC):
                    dve.tensor_scalar(tile(a_t, c, T), bank(2, c), vec[:, C_GAMMA + c:C_GAMMA + c + 1],
                                      vec[:, C_BETA + c:C_BETA + c + 1], ALU.mult, ALU.add).then_inc(a_done, 1)

            def a_low(n):
                dve.wait_ge(a_hi_done, DC * (n + 1))
                dve.tensor_tensor(a_lo, a_t, f32(a_hi), ALU.subtract).then_inc(a_lo_done, 1)

            def relu_half(n, q):
                j = NQ * n + q
                dve.wait_ge(w1_done, j + 1)
                after(dve, hid_lo_done, j - 1)
                dve.tensor_scalar(hid[q % 2][:, 0:512], bank(HP[q], 0), vec[:, C_B1 + 2 * q:C_B1 + 2 * q + 1], 0.0,
                                  ALU.add, ALU.max).then_inc(relu_dve_done, 1)

            dve.memset(ek_rows, 0.0).then_inc(const_set, 1)
            dve.memset(xn_t[:, 0:1], 0.0).then_inc(const_set, 1)
            dve.memset(xn_t[:, T + 1:T + 2], 0.0).then_inc(const_set, 1)
            head_stats(0)
            dve.wait_ge(nmr_done["head"], 1)
            normalise_tiles("head", x_in, range(TT - FIRST_DVE, TT))
            dve.wait_ge(ctx_landed, 16)
            dve.wait_ge(norm_done["head"], TT)
            for h in range(2):
                v = tile(emb[0], h, 2 * D)
                dve.tensor_tensor(v, tile(norm, h, 2 * D), v, ALU.add
                                  ).then_inc(*((emb_half_done, 1) if h == 0 else (emb_done, 1)))
            unit_low(0)
            pos_max(0)
            emb_low(0)
            unit_low(1)
            head_stats(1)
            key_max(0)
            pos_max(1)
            dve.wait_ge(const_set, 3)
            sum_keys(0)
            dve.wait_ge(far_landed, 16)
            dve.wait_ge(c_col_done, 2)
            for a in range(TT):
                v = tile(far_in, TT + a, FAR)
                dve.tensor_scalar(v, v, c_col[:, a:a + 1], None, ALU.mult).then_inc(far_masked, 1)
            keep_values(0, 3)
            dve.wait_ge(act_const, 3)
            dve.wait_ge(rows_landed, 16 * 5)
            dve.tensor_tensor(bias_rows, bias_rows, beta_t, ALU.add).then_inc(dve_const, 1)
            dve.tensor_scalar(gamma_t, gamma_t, gates[:, 0:1], None, ALU.mult).then_inc(dve_const, 1)
            dve.wait_ge(dve_const, 2)
            dve.tensor_scalar(beta_t, beta_t, gates[:, 0:1], None, ALU.mult).then_inc(dve_const, 1)
            dve.tensor_scalar(gates[:, 1:2], gates[:, 2:3], 0.5, None, ALU.mult).then_inc(dve_const, 1)
            for j in range(TT):
                if j == TT // 2:
                    keys_low(0)
                dve.wait_ge(ew_hi_done, j + 1)
                dve.tensor_tensor(tile(ew_lo, j, WIN), ew_window(j), f32(tile(ew_hi, j, WIN)), ALU.subtract
                                  ).then_inc(ew_lo_done, 1)
            dve.wait_ge(far_hi_done, 1)
            dve.tensor_tensor(far_c[32:64], bank(1, 1)[32:64], f32(far_c)[32:64], ALU.subtract).then_inc(far_lo_done, 1)
            weigh_values(0)
            dve.wait_ge(dve_const, 4)

            def step(i, p):
                a, b, d, e = i - 2, i - 1, i + 1, i + 2
                first = isinstance(i, int) and i == 0
                sums_low(i, 0)
                recip(i, 0)
                if has(a):
                    mix_k(a, [0])
                sums_low(i, 1)
                if has(a):
                    mix_k(a, [1])
                if has(d):
                    emb_low(d)
                recip(i, 1)
                if has(a):
                    mix_r(a)
                make_y(i)
                if first:
                    unit_low(2)
                    y_low(dve, i)
                if has(a):
                    square(a)
                if has(d) and not first:
                    key_max(d)
                if isinstance(i, int) and i == 1:
                    unit_low(6)
                    unit_low(7)
                if has(b):
                    relu_half(b, 2)
                if has(d) and not first:
                    sum_keys(d)
                if first:
                    first_attention_sum()
                else:
                    attention_sum(i, p)
                if first:
                    key_max(d, 3)
                    dve.wait_ge(emb_done, 2)
                    dve.wait_ge(nmr_done["mid"], 1)
                    normalise_tiles("mid", res, range(TT - FIRST_DVE, TT))
                    unit_low(3)
                if has(b):
                    relu_half(b, 3)
                if has(a):
                    gate_ffn(a)
                    make_out(a)
                if has(e) and not first:
                    head_stats(e)
                if has(b):
                    ff_sum(b, 1 - p)
                make_a(i)
                if first:
                    head_stats(e)
                if has(b):
                    ff_stats(b, lambda: a_low(i))
                else:
                    a_low(i)
                if first:
                    unit_low(4)
                    unit_low(5)
                if has(b):
                    scale_ff(b)
                relu_half(i, 0)
                if first:
                    sum_keys(d)
                if has(b):
                    finish_x1(b)
                    fin_stats(b)
                relu_half(i, 1)
                if has(d):
                    keep_values(d)
                if has(b):
                    normalise_fin(b)
                if has(d):
                    keys_low(d)
                    weigh_values(d)

            run_steps(dve, step)
            a, b = BATCH - 2, BATCH - 1
            relu_half(b, 2)
            delta_of(dve, a)
            mix_k(a)
            xk_low(dve, a)
            relu_half(b, 3)
            mix_r(a)
            dve.wait_ge(w2_done, NQ * b + 3)
            hidden_low(dve, b, 3)
            ff_sum(b, b % 2)
            ff_stats(b)
            scale_ff(b)
            finish_x1(b)
            fin_stats(b)
            sq_low(dve, a)
            normalise_fin(b)
            dve.wait_ge(sq_lo_done, a + 1)
            delta_of(dve, b)
            mix_k(b)
            mix_r(b, [0])
            xk_low(dve, b)
            mix_r(b, [1])
            gate_ffn(a)
            xr_low(dve, b)
            square(b)
            make_out(a)
            sq_low(dve, b)
            for h in range(2):
                gate_ffn(b, 2, h)
                make_out(b, 2, h)

        @block.scalar
        def _(act):
            def normalise_tile(kind, src, a):
                act.activation(tile(norm, a), tile(src, a), ACT.Identity, bias=nmr[kind][:, a:a + 1],
                               scale=rs[kind][:, a:a + 1]).then_inc(norm_done[kind], 1)

            def normalise(kind, n, src):
                if kind == "head":
                    after(act, mid_turned, n - 1)
                    after(act, a_scaled_done, n - 1)
                    after(act, emb_done, n)
                elif kind == "mid":
                    after(act, fin_turned, DC * (n - 1))
                    after(act, emb_done, most(n + 2, BATCH))
                else:
                    act.wait_ge(mid_turned, most(n + 2, BATCH))
                    act.wait_ge(a_scaled_done, most(n + 2, BATCH))
                    act.wait_ge(emb_done, most(n + 4, BATCH))
                act.wait_ge(nmr_done[kind], n + 1)
                short = kind == "mid" and isinstance(n, int) and n == 0
                for a in range(FIN_DVE if kind == "fin" else 0, TT - FIRST_DVE if short else TT):
                    normalise_tile(kind, src, a)

            def unit_high(u):
                act.wait_ge(unit_landed[u], unit_count(u))
                n = unit_cols[u]
                act.activation(w_hi[u][:, :n], stage[UNIT_STAGE[u]][:, :n], ACT.Copy).then_inc(w_hi_done, 1)

            def emb_high(n):
                act.wait_ge(emb_turned, n + 1)
                act.activation(emb_hi, pair(0), ACT.Copy).then_inc(emb_hi_done, 1)

            def exp_keys(n, src=1):
                act.wait_ge(kbias_done, n + 1)
                after(act, y_lo_done, n)
                for c in range(DC):
                    act.activation(tile(ek_t, c, T), bank(src, c), ACT.Exp, bias=kbias[:, c:c + 1]).then_inc(ek_done, 1)

            def tanh_q(n, src=1):
                act.wait_ge(q_done, n + 1)
                after(act, y_done, DC * n)
                for c in range(DC):
                    act.activation(tile(gate_q, c, T), bank(src, c), ACT.Tanh, bias=half_bq[:, c:c + 1], scale=0.5
                                   ).then_inc(tanh_q_done, 1)

            def sigmoid_q(n):
                act.wait_ge(tanh_q_done, DC * (n + 1))
                act.activation(gate_q, gate_q, ACT.Copy, bias=0.5, scale=0.5).then_inc(gate_q_done, 1)

            def ek_high(n):
                act.wait_ge(ek_turned, n + 1)
                after(act, wo_done, n)
                act.activation(ek_hi, pair(0), ACT.Copy).then_inc(ek_hi_done, 1)

            def key_sums_high(n):
                act.wait_ge(sums_done, 2 * n + 1)
                after(act, num_done, DC * n)
                act.activation(sums_r[0:FAR], bank(2, 0, D)[0:FAR], ACT.Copy).then_inc(sums_hi_done, 1)

            def keep_sums(n):
                act.wait_ge(sums_done, 2 * n + 2)
                after(act, sums_lo_done, 2 * n)
                act.activation(sums[0:FAR], bank(2, 1, D)[0:FAR], ACT.Copy).then_inc(sums_kept, 1)
                act.wait_ge(den_done, DC * (n + 1))
                act.wait_ge(sums_kept, n + 1)
                act.activation(sums_r[0:FAR], sums[0:FAR], ACT.Copy).then_inc(sums_hi_done, 1)

            def ev_high(n):
                act.wait_ge(ev_done, n + 1)
                after(act, fv_done, n - 2)
                act.activation(ev_hi, val, ACT.Copy).then_inc(ev_hi_done, 1)

            def turned_copy(n):
                after(act, xr_done, DC * n)
                for c in range(DC):
                    o = c * (T + 1) + 1
                    act.wait_ge(fin_turned, DC * n + c + 1)
                    act.activation(xn_t[:, o:o + T], bank(2, c), ACT.Copy).then_inc(xn_t_done, 1)

            def mixed_high(n):
                for c in range(DC):
                    act.wait_ge(xk_done, DC * n + c + 1)
                    act.activation(tile(xk_hi, c, T), tile(xk, c, T), ACT.Copy).then_inc(xk_hi_done, 1)

            def mixed_r_high(n):
                act.wait_ge(xr_done, DC * (n + 1))
                act.activation(xr_hi, xr_of(n), ACT.Copy).then_inc(xr_hi_done, 1)

            def relu_k(n):
                act.wait_ge(fk_done, n + 1)
                act.wait_ge(xk_lo_done, n + 1)
                act.activation(xk, pair(key_pair(n)), ACT.Relu).then_inc(relu_k_done, 1)

            def tanh_r(n):
                act.wait_ge(fr_done, n + 1)
                act.activation(xr_of(n), pair(2), ACT.Tanh, scale=0.5).then_inc(tanh_r_done, 1)

            def square_high(n):
                act.wait_ge(sq_done, n + 1)
                act.wait_ge(num_done, most(DC * (n + 3), DC * BATCH))
                act.activation(sq_hi, xk, ACT.Copy).then_inc(sq_hi_done, 1)

            def y_high(n):
                act.wait_ge(y_done, DC * (n + 1))
                act.activation(y_hi, y, ACT.Copy).then_inc(y_hi_done, 1)

            def a_high(n):
                after(act, w1_done, NQ * n)
                for c in range(DC):
                    act.wait_ge(a_done, DC * n + c + 1)
                    act.activation(tile(a_hi, c, T), tile(a_t, c, T), ACT.Copy).then_inc(a_hi_done, 1)

            def relu_half(n, q):
                j = NQ * n + q
                act.wait_ge(w1_done, j + 1)
                after(act, hid_lo_done, j - 1)
                act.activation(hid[q % 2][:, 512:PAIR], bank(HP[q], 1), ACT.Relu,
                               bias=vec[:, C_B1 + 2 * q + 1:C_B1 + 2 * q + 2]).then_inc(relu_act_done, 1)

            def hidden_high(n, q):
                j = NQ * n + q
                after(act, w2_done, j - 1)
                act.wait_ge(relu_dve_done, j + 1)
                act.wait_ge(relu_act_done, j + 1)
                act.activation(hid_hi[q % 2], hid[q % 2], ACT.Copy).then_inc(hid_hi_done, 1)

            act.wait_ge(ident_set, 2)
            act.activation(c_col, ident[:, 0:TT], ACT.Tanh).then_inc(c_col_done, 1)
            act.wait_ge(x_landed, 16)
            for u in range(2):
                act.dma_start(stage[2 + u].rearrange("p (a j) -> p a j", a=2),
                              A_pos.rearrange("(a p) j -> p a j", p=P)[:, 2 * u:2 * u + 2]).then_inc(pos_landed[u], 16)
            load_unit(act, 1)
            act.wait_ge(nmr_done["head"], 1)
            for a in range(TT - FIRST_DVE):
                normalise_tile("head", x_in, a)
            unit_high(0)
            emb_high(0)
            act.wait_ge(vec_landed, 16)
            act.activation(half_bq, vec[:, C_BQ:C_BQ + DC], ACT.Copy, scale=0.5).then_inc(act_const, 1)
            act.activation(gates[:, 0:1], vec[:, C_GX:C_GX + 1], ACT.Tanh).then_inc(act_const, 1)
            act.activation(gates[:, 2:3], vec[:, C_GF:C_GF + 1], ACT.Tanh).then_inc(act_const, 1)
            unit_high(1)
            act.wait_ge(far_landed, 16)
            act.activation(tile_rows, far_in[:, 0:TT * FAR], ACT.Copy).then_inc(tile_rows_done, 1)
            for u in range(2):
                act.wait_ge(pos_max_done, u + 1)
                for a in range(2):
                    v = tile(stage[2 + u], a, T)
                    act.activation(v, v, ACT.Exp, bias=pos_nmax[:, 2 * u + a:2 * u + a + 1]).then_inc(pos_exp_done, 1)
                if u == 0:
                    unit_high(2)
                    exp_keys(0)
            act.wait_ge(c_col_done, 1)
            act.activation(c_col, pos_nmax, ACT.Exp).then_inc(c_col_done, 1)
            act.wait_ge(act_const, 1)
            tanh_q(0, 2)
            ek_high(0)
            for j in range(TT):
                act.wait_ge(pos_turned, j // 2 + 1)
                act.activation(tile(ew_hi, j, WIN), ew_window(j), ACT.Copy).then_inc(ew_hi_done, 1)
            act.wait_ge(far_turned, 1)
            act.activation(far_c[0:FAR], bank(1, 1)[0:FAR], ACT.Copy).then_inc(far_hi_done, 1)
            normalise("head", 1, x_in)
            key_sums_high(0)
            ev_high(0)
            sigmoid_q(0)
            unit_high(3)

            def step(i, p):
                a, b, d, e = i - 2, i - 1, i + 1, i + 2
                first = isinstance(i, int) and i == 0
                if first:
                    unit_high(4)
                if has(b):
                    hidden_high(b, 1)
                if has(d):
                    after(act, v_done, d)
                    emb_high(d)
                keep_sums(i)
                if isinstance(i, int) and i == 1:
                    unit_high(6)
                    unit_high(7)
                if has(a):
                    mixed_high(a)
                if first:
                    unit_high(5)
                if has(a):
                    mixed_r_high(a)
                    relu_k(a)
                y_high(i)
                if has(a):
                    square_high(a)
                    tanh_r(a)
                if first:
                    tanh_q(d)
                if has(d) and not first:
                    exp_keys(d)
                if has(b):
                    relu_half(b, 2)
                    hidden_high(b, 2)
                if has(b):
                    relu_half(b, 3)
                    hidden_high(b, 3)
                normalise("mid", i, res)
                if first:
                    exp_keys(d, 3)
                a_high(i)
                if has(e):
                    normalise("head", e, x_in)
                if has(d) and not first:
                    tanh_q(d)
                relu_half(i, 0)
                hidden_high(i, 0)
                relu_half(i, 1)
                if is_last(i):
                    hidden_high(i, 1)
                if has(b):
                    normalise("fin", b, x1)
                if has(d):
                    ek_high(d)
                if has(b) and not is_last(i):
                    turned_copy(b)
                if has(d):
                    key_sums_high(d)
                    ev_high(d)
                    sigmoid_q(d)

            run_steps(act, step)
            a, b = BATCH - 2, BATCH - 1
            relu_half(b, 2)
            hidden_high(b, 2)
            turned_copy(a)
            mixed_high(a)
            relu_half(b, 3)
            hidden_high(b, 3)
            act.wait_ge(w2_done, NQ * b + 3)
            mixed_r_high(a)
            relu_k(a)
            tanh_r(a)
            square_high(a)
            normalise("fin", b, x1_of(b))
            turned_copy(b)
            mixed_high(b)
            mixed_r_high(b)
            relu_k(b)
            square_high(b)
            tanh_r(b)

        @block.tensor
        def _(pe):
            def mm(o, s, m, start, stop):
                return pe.matmul(o, s, m, start=start, stop=stop, skip_group_check=True)

            def turn(dst, src, done, by_chunk=False):
                for c in range(DC):
                    for a in range(TT):
                        last = pe.transpose(bank(dst, c)[:, a * P:(a + 1) * P],
                                            src[:, D * a + c * P:D * a + (c + 1) * P], ident)
                    if by_chunk or c == DC - 1:
                        last.then_inc(done, 1)

            def turn_back(dst, src, done):
                for a in range(TT):
                    for c in range(DC):
                        last = pe.transpose(tile(pair(dst), a)[:, c * P:(c + 1) * P],
                                            src[:, T * c + a * P:T * c + (a + 1) * P], ident)
                last.then_inc(done, 1)

            def unit(u, k):
                return w_hi[u][:, 512 * k:512 * (k + 1)], w_lo[u][:, 512 * k:512 * (k + 1)]

            def channels_out(dst, w, act_hi, act_lo, lo_ready, lo_count, done, hi_ready=None, hi_count=0):
                hi, lo = w
                for k in range(DC):
                    if hi_ready is not None:
                        pe.wait_ge(hi_ready, hi_count + k + 1)
                    for c in range(DC):
                        for r in (hi, lo):
                            mm(bank(dst, c), r[:, D * k + c * P:D * k + (c + 1) * P], tile(act_hi, k, T),
                               k == 0 and r is hi, False)
                pe.wait_ge(lo_ready, lo_count)
                for c in range(DC):
                    for k in range(DC):
                        last = mm(bank(dst, c), hi[:, D * k + c * P:D * k + (c + 1) * P], tile(act_lo, k, T),
                                  False, k == DC - 1)
                last.then_inc(done, 1)

            def rows_out(dst, w, act_hi, act_lo, lo_ready, lo_count, done, half_done=None, between=None):
                hi, lo = w

                def high_part(tiles):
                    for a in tiles:
                        o = tile(pair(dst), a)
                        for k in range(DC):
                            s = act_hi[:, T * k + a * P:T * k + (a + 1) * P]
                            mm(o, s, tile(hi, k), a % 2 == 0 and k == 0, False)
                            mm(o, s, tile(lo, k), False, False)

                def low_part(tiles):
                    for a in tiles:
                        o = tile(pair(dst), a)
                        for k in range(DC):
                            s = act_lo[:, T * k + a * P:T * k + (a + 1) * P]
                            last = mm(o, s, tile(hi, k), False, a % 2 == 1 and k == DC - 1)
                    return last

                if half_done is None:
                    high_part(range(TT))
                    pe.wait_ge(lo_ready, lo_count)
                    low_part(range(TT)).then_inc(done, 1)
                else:
                    high_part(range(TT // 2))
                    pe.wait_ge(lo_ready, lo_count)
                    low_part(range(TT // 2)).then_inc(half_done, 1)
                    if between is not None:
                        between()
                    high_part(range(TT // 2, TT))
                    low_part(range(TT // 2, TT)).then_inc(done, 1)

            def relus_read(count):
                after(pe, relu_dve_done, count)
                after(pe, relu_act_done, count)

            def turn_emb(n, p):
                pe.wait_ge(emb_done, n + 1)
                after(pe, ev_done, n)
                turn(0, emb[p], emb_turned)

            def keys(n, dst=1):
                pe.wait_ge(emb_hi_done, n + 1)
                if dst == 1:
                    after(pe, recip_done, DC * n)
                channels_out(dst, unit(0, 0), emb_hi, emb_lo, emb_lo_done, n + 1, k_done)

            def queries(n, dst=1, keys_in=1):
                if keys_in != 1:
                    pe.wait_ge(recip_done, DC * n)
                elif dst == 1:
                    pe.wait_ge(ek_done, DC * (n + 1))
                    relus_read(NQ * (n - 1))
                channels_out(dst, unit(0, 1), emb_hi, emb_lo, emb_lo_done, n + 1, q_done)

            def values(n, dst=1):
                if dst == 1:
                    pe.wait_ge(tanh_q_done, DC * (n + 1))
                rows_out(dst, unit(1, 0), emb_hi, emb_lo, emb_lo_done, n + 1, v_done)

            def turn_keys(n):
                pe.wait_ge(emb_lo_done, n + 1)
                relus_read(NQ * (n - 1) + 1)
                turn_back(0, ek_t, ek_turned)

            def near(dst, c, part, ew, first=False):
                for j in range(TT):
                    o = bank(dst, c)[:, window(j):window(j) + WIN]
                    for w in ew:
                        mm(o, part[:, D * j + c * P:D * j + (c + 1) * P], tile(w, j, WIN),
                           first and j == 0 and w is ew[0], False)

            def weigh(n, part, dst, hi, lo, lo_ready, done):
                opening = isinstance(n, int) and n == 0 and part == 0
                if opening:
                    pe.wait_ge(ew_hi_done, TT)
                    near(dst, 0, hi, (ew_hi,), True)
                    pe.wait_ge(ew_lo_done, TT)
                    near(dst, 0, hi, (ew_lo,))
                else:
                    near(dst, 0, hi, (ew_hi, ew_lo), True)
                if part == 0:
                    pe.wait_ge(lo_ready, n + 1)
                    near(dst, 0, lo, (ew_hi,))
                    after(pe, xn_t_done, DC * (n - 1))
                    relus_read(NQ * (n - 1) + 2)
                    pe.wait_ge(ek_rows_done, n + 1)
                    for c in range(DC):
                        last = pe.transpose(bank(2, 0)[0:FAR, c * P:(c + 1) * P], ek_rows[:, 96 * c:96 * c + FAR], ident)
                else:
                    o = bank(2, 1, D)[0:FAR]
                    for p in (hi, lo):
                        if p is lo:
                            pe.wait_ge(lo_ready, n + 1)
                        for j in range(TT):
                            last = mm(o, tile(tile_rows, j, FAR), tile(p, j), p is hi and j == 0, p is lo and j == TT - 1)
                last.then_inc(sums_done, 1)
                if part == 1:
                    near(dst, 0, lo, (ew_hi,))
                    pe.wait_ge(sums_kept, n + 1)
                if opening:
                    pe.wait_ge(tile_rows_done, 1)
                    pe.wait_ge(far_lo_done, 1)
                near(dst, 1, hi, (ew_hi, ew_lo), True)
                near(dst, 1, lo, (ew_hi,))
                pe.wait_ge(sums_hi_done, 2 * n + part + 1)
                pe.wait_ge(sums_lo_done, 2 * n + part + 1)
                for c in range(DC):
                    mm(bank(dst, c), sums_r[0:FAR, c * P:(c + 1) * P], far_c[0:FAR], False, True).then_inc(done, 1)

            def hidden(n, q, hi_count=None):
                for k in range(DC):
                    if hi_count is not None:
                        pe.wait_ge(a_hi_done, hi_count + k + 1)
                    for b in range(2):
                        m = 2 * q + b
                        for w in (w_hi, w_lo):
                            mm(bank(HP[q], b), w[2 + k][:, m * P:(m + 1) * P], tile(a_hi, k, T), k == 0 and w is w_hi, False)
                pe.wait_ge(a_lo_done, n + 1)
                for b in range(2):
                    m = 2 * q + b
                    for k in range(DC):
                        last = mm(bank(HP[q], b), w_hi[2 + k][:, m * P:(m + 1) * P], tile(a_lo, k, T), False, k == DC - 1)
                last.then_inc(w1_done, 1)

            def add_hidden(n, q):
                r = q % 2

                def add(part, act_part, a, last_part):
                    for b in range(2):
                        m = 2 * q + b
                        s = act_part[:, T * b + a * P:T * b + (a + 1) * P]
                        for w in part:
                            o = mm(tile(pair(3), a), s, tile(w[4 + m // 4], m % 4),
                                   q == 0 and a % 2 == 0 and b == 0 and part is hi_lo and w is w_hi,
                                   last_part and q == NQ - 1 and a % 2 == 1 and b == 1)
                    return o

                hi_lo, hi_only = (w_hi, w_lo), (w_hi,)
                if q == 0:
                    after(pe, ff_sum_done, DC * n)
                pe.wait_ge(hid_hi_done, NQ * n + q + 1)
                for a in range(TT):
                    add(hi_lo, hid_hi[r], a, False)
                pe.wait_ge(hid_lo_done, NQ * n + q + 1)
                for a in range(TT):
                    last = add(hi_only, hid_lo[r], a, True)
                    if q == NQ - 1 and a == TT // 2 - 1:
                        last.then_inc(ff_half_done, 1)
                last.then_inc(w2_done, 1)

            def turn_fin(n):
                pe.wait_ge(norm_done["fin"], TT * (n + 1))
                relus_read(most(NQ * (n + 1) + 2, NQ * BATCH))
                turn(2, norm, fin_turned, by_chunk=True)

            def ffn_k(n):
                pe.wait_ge(emb_lo_done, most(n + 4, BATCH))
                channels_out(key_pair(n), unit(6, 0), xk_hi, xk_lo, xk_lo_done, n + 1, fk_done, xk_hi_done, DC * n)

            def ffn_r(n):
                pe.wait_ge(ratio_done, most(DC * (n + 3), DC * BATCH))
                pe.wait_ge(xn_t_done, DC * (n + 1))
                pe.wait_ge(xr_hi_done, n + 1)
                rows_out(2, unit(6, 1), xr_hi, xr_lo, xr_lo_done, n + 1, fr_done)

            def ffn_v(n, between=None):
                pe.wait_ge(sq_hi_done, n + 1)
                relus_read(most(NQ * (n + 1) + 3, NQ * BATCH))
                rows_out(0, unit(7, 0), sq_hi, sq_lo, sq_lo_done, n + 1, fv_done,
                         fv_half_done if isinstance(n, int) and n >= BATCH - 2 else None, between)

            pe.wait_ge(ident_set, 2)
            for h in range(2):
                pe.wait_ge(*((emb_half_done, 1) if h == 0 else (emb_done, 1)))
                for c in range(DC):
                    for a in range(2 * h, 2 * h + 2):
                        last = pe.transpose(bank(0, c)[:, a * P:(a + 1) * P],
                                            emb[0][:, D * a + c * P:D * a + (c + 1) * P], ident)
            last.then_inc(emb_turned, 1)
            pe.wait_ge(w_lo_done, 1)
            keys(0)
            queries(0, 2)
            pe.wait_ge(w_lo_done, 2)
            values(0, 3)
            pe.wait_ge(ek_done, DC)
            turn_keys(0)
            pe.wait_ge(pos_exp_done, TT)
            for u in range(2):
                pe.wait_ge(*((tanh_q_done, DC) if u == 0 else (val_done, 1)))
                for b in range(2):
                    for a in range(TT):
                        j = 2 * u + b
                        last = pe.transpose(bank(2 + u, b)[:, a * P:(a + 1) * P],
                                            stage[2 + a // 2][:, T * (a % 2) + j * P:T * (a % 2) + (j + 1) * P], ident)
                last.then_inc(pos_turned, 1)
            pe.wait_ge(far_masked, TT)
            for a in range(TT):
                last = pe.transpose(bank(1, 1)[0:FAR, a * P:(a + 1) * P], tile(far_in, TT + a, FAR), ident)
            last.then_inc(far_turned, 1)

            def step(i, p):
                a, b, d = i - 2, i - 1, i + 1
                first = isinstance(i, int) and i == 0
                pe.wait_ge(ek_hi_done, i + 1)
                pe.wait_ge(val_done, i + 1)
                weigh(i, 0, 1, ek_hi, ek_lo, ek_lo_done, den_done)
                if has(d):
                    turn_emb(d, 1 - p)
                pe.wait_ge(ev_hi_done, i + 1)
                pe.wait_ge(sums_lo_done, 2 * i + 1)
                weigh(i, 1, 2, ev_hi, ev_lo, ev_lo_done, num_done)
                if has(b):
                    add_hidden(b, 1)
                if has(a):
                    if isinstance(a, int) and a == 0:
                        pe.wait_ge(w_lo_done, NU)
                    ffn_k(a)
                if first:
                    keys(d, 3)
                    queries(d, keys_in=3)
                elif has(d):
                    keys(d)
                if has(a):
                    ffn_r(a)
                if has(b):
                    if has(a):
                        pe.wait_ge(sq_done, a + 1)
                    pe.wait_ge(emb_lo_done, most(b + 3, BATCH))
                    hidden(b, 2)
                if has(a):
                    pe.wait_ge(tanh_r_done, a + 1)
                pe.wait_ge(y_hi_done, i + 1)
                rows_out(2, unit(1, 1), y_hi, y_lo, y_lo_done, i + 1, wo_done, wo_half_done if first else None)
                if has(b):
                    pe.wait_ge(ek_done, most(DC * (b + 3), DC * BATCH))
                    pe.wait_ge(recip_done, most(DC * (b + 2), DC * BATCH))
                    hidden(b, 3)
                if has(a):
                    ffn_v(a)
                if has(b):
                    add_hidden(b, 2)
                    add_hidden(b, 3)
                if first:
                    values(d)
                pe.wait_ge(norm_done["mid"], TT * (i + 1))
                turn(2, norm, mid_turned)
                if has(d) and not first:
                    queries(d)
                if has(a):
                    pe.wait_ge(gated_done, a + 1)
                relus_read(NQ * i - 1)
                if first:
                    pe.wait_ge(w_lo_done, 4)
                    pe.wait_ge(emb_lo_done, 2)
                hidden(i, 0, DC * i)
                hidden(i, 1)
                if has(d):
                    if not first:
                        values(d)
                    turn_keys(d)
                if first:
                    pe.wait_ge(w_lo_done, 5)
                    pe.wait_ge(ek_done, DC * 2)
                add_hidden(i, 0)
                if is_last(i):
                    relus_read(NQ * i + 1)
                    hidden(i, 2)
                if has(b):
                    turn_fin(b)

            run_steps(pe, step)
            a, b = BATCH - 2, BATCH - 1
            add_hidden(b, 1)
            pe.wait_ge(recip_done, DC * BATCH)
            hidden(b, 3)
            add_hidden(b, 2)
            add_hidden(b, 3)
            relus_read(NQ * b + 3)
            ffn_k(a)
            ffn_r(a)
            pe.wait_ge(sq_done, a + 1)
            pe.wait_ge(tanh_r_done, a + 1)
            ffn_v(a, lambda: turn_fin(b))
            pe.wait_ge(relu_act_done, NQ * BATCH)
            pe.wait_ge(relu_dve_done, NQ * BATCH)
            ffn_k(b)
            ffn_r(b)
            pe.wait_ge(gated_done, a + 1)
            ffn_v(b)


_SHAPE = (BATCH, T, D)


def kernel(x, ctx_1024, g_xattn, g_ffn, L0_xattn_wq, L0_xattn_bq, L0_xattn_wk, L0_xattn_bk, L0_xattn_wv, L0_xattn_bv,
           L0_xattn_wo, L0_xattn_bo, L0_xattn_pos_bias, L0_xattn_gamma, L0_xattn_beta, L0_xattn_w1, L0_xattn_b1,
           L0_xattn_w2, L0_xattn_b2, L0_ffn_W_r, L0_ffn_W_k, L0_ffn_W_v, L0_ffn_mu_r, L0_ffn_mu_k):
    import numpy as np
    import concourse.bacc as bacc
    from concourse.bass_utils import run_bass_kernel_spmd

    def columns(v):
        return np.asarray(v).reshape(-1, P).T

    vec = np.concatenate([columns(v) for v in (L0_xattn_bq, L0_xattn_bk, L0_xattn_bv, L0_xattn_gamma, L0_xattn_beta,
                                               L0_ffn_mu_r, L0_ffn_mu_k, L0_xattn_b1)]
                         + [np.broadcast_to(np.asarray(g).reshape(1, 1), (P, 1)) for g in (g_xattn, g_ffn)], axis=1)
    rows = np.broadcast_to(np.concatenate([np.asarray(v) for v in (L0_xattn_gamma, L0_xattn_beta, L0_xattn_bo, L0_xattn_b2)])[None, :],
                           (P, 4 * D))
    far = np.zeros((P, 2, TT, FAR), np.float32)
    for j in range(TT):
        outside = (np.arange(T) < window(j)) | (np.arange(T) >= window(j) + WIN)
        for k in range(3):
            far[:, 0, j, 32 * k + j] = 1
            far[:, 1, :, 32 * k + j] = outside.reshape(TT, P).T
    named = {
        "x": x, "ctx": ctx_1024, "vec": vec, "rows": rows, "far": far.reshape(P, -1), "pos": L0_xattn_pos_bias,
        "wk": L0_xattn_wk, "wq": L0_xattn_wq, "wv": L0_xattn_wv, "wo": L0_xattn_wo, "w1": L0_xattn_w1, "w2": L0_xattn_w2,
        "fk": np.asarray(L0_ffn_W_k).T, "fr": np.asarray(L0_ffn_W_r).T, "fv": np.asarray(L0_ffn_W_v).T,
    }
    nc = bacc.Bacc("TRN2", target_bir_lowering=False, num_devices=1)
    arrays, args = {}, []
    for name, a in named.items():
        a = np.ascontiguousarray(a)
        arrays[f"in_{name}"] = a
        args.append(nc.dram_tensor(f"in_{name}", a.shape, mybir.dt.from_np(a.dtype), kind="ExternalInput").ap())
    args.append(nc.dram_tensor("out_0", _SHAPE, F32, kind="ExternalOutput").ap())
    flamingo_gated_block(nc, *args)
    r = run_bass_kernel_spmd(nc, [arrays], core_ids=[0])
    return r.results[0]["out_0"]
```
